# Optimizing a Trainium2 kernel written in Bass

```python
import numpy as np
import jax
import jax.numpy as jnp

def _softmax(x, axis=-1):
    return jax.nn.softmax(x, axis=axis)

def _gelu(x):
    return jax.nn.gelu(x, approximate=True)

def _silu(x):
    return jax.nn.silu(x)

def _sigmoid(x):
    return jax.nn.sigmoid(x)

def _layernorm(x, axis=-1, eps=1e-05):
    m = jnp.mean(x, axis=axis, keepdims=True)
    v = jnp.var(x, axis=axis, keepdims=True)
    return (x - m) / jnp.sqrt(v + eps)

def _scatter_add(tgt, idx, src, axis=0):
    return tgt.at[idx].add(src)

def _segment_sum(src, seg, n):
    return jax.ops.segment_sum(src, seg, n)
kernel_name = 'mk_hybrid_d1_jaxref_r8_f5436a'

def setup_inputs(seed: int=0):
    np.random.seed(seed)
    _w = jnp.asarray

    def _L0_attn_a_setup():
        import jax, jax.numpy as jnp
        import numpy as np
        D_MODEL = 256
        NUM_HEADS = 16
        D_HEAD = D_MODEL // NUM_HEADS
        key = jax.random.key(seed)
        kx, kq, kk, kv, ko = jax.random.split(key, 5)
        std = np.sqrt(2.0 / (D_MODEL + D_MODEL)).astype(np.float32)

        def tn(k):
            return std * jax.random.truncated_normal(k, -3.0, 3.0, (D_MODEL, D_MODEL), dtype=jnp.float32)
        return {'x': jax.random.normal(kx, (4, 256, D_MODEL), dtype=jnp.float32), 'w_q': tn(kq), 'w_k': tn(kk), 'w_v': tn(kv), 'w_o': tn(ko)}
    _L0_attn_a_in = _L0_attn_a_setup()

    def _L0_attn_b_setup():
        import jax, jax.numpy as jnp
        import numpy as np
        L, N, E, H = (256, 2, 256, 16)
        DH = E // H
        SCALE = DH ** (-0.5)
        key = jax.random.key(seed)
        k1, k2, k3 = jax.random.split(key, 3)
        x = jax.random.normal(k1, (L, N, E), dtype=jnp.float32)
        weight_qkv = jax.random.normal(k2, (3 * E, E), dtype=jnp.float32) * 0.02
        weight_out = jax.random.normal(k3, (E, E), dtype=jnp.float32) * 0.02
        return {'x': x, 'weight_qkv': weight_qkv, 'weight_out': weight_out}
    _L0_attn_b_in = _L0_attn_b_setup()

    def _L0_ffn_setup():
        import jax, jax.numpy as jnp
        import numpy as np
        HIDDEN = 256
        INTER = 1024
        SCALE = 64.0

        def fwht(x):
            orig_shape = x.shape
            n = orig_shape[-1]
            x = x.reshape(-1, n)
            h = 1
            while h < n:
                x = x.reshape(-1, n // (2 * h), 2, h)
                a, b = (x[:, :, 0, :], x[:, :, 1, :])
                x = jnp.stack([a + b, a - b], axis=2).reshape(-1, n)
                h *= 2
            return (x / jnp.sqrt(jnp.asarray(n, x.dtype))).reshape(orig_shape)
        key = jax.random.key(seed)
        ks = jax.random.split(key, 8)
        inp = jax.random.normal(ks[0], (4, 256, HIDDEN), dtype=jnp.float32)
        SU_ug = jnp.where(jax.random.bernoulli(ks[1], 0.5, (HIDDEN,)), 1.0, -1.0).astype(jnp.float32)
        SU_dp = jnp.where(jax.random.bernoulli(ks[2], 0.5, (INTER,)), 1.0, -1.0).astype(jnp.float32)
        Wscale_ug = jax.random.uniform(ks[3], (2 * INTER,), jnp.float32, 0.5, 1.5)
        Wscale_dp = jax.random.uniform(ks[4], (HIDDEN,), jnp.float32, 0.5, 1.5)
        W_up = jax.random.normal(ks[5], (INTER, HIDDEN), dtype=jnp.float32) * 0.02
        W_gate = jax.random.normal(ks[6], (INTER, HIDDEN), dtype=jnp.float32) * 0.02
        W_down = jax.random.normal(ks[7], (HIDDEN, INTER), dtype=jnp.float32) * 0.02
        return {'input': inp, 'SU_ug': SU_ug, 'SU_dp': SU_dp, 'Wscale_ug': Wscale_ug, 'Wscale_dp': Wscale_dp, 'W_up': W_up, 'W_gate': W_gate, 'W_down': W_down}
    _L0_ffn_in = _L0_ffn_setup()
    _d = {'L0_attn_a_x': _L0_attn_a_in['x'], 'L0_attn_a_w_q': _L0_attn_a_in['w_q'], 'L0_attn_a_w_k': _L0_attn_a_in['w_k'], 'L0_attn_a_w_v': _L0_attn_a_in['w_v'], 'L0_attn_a_w_o': _L0_attn_a_in['w_o'], 'L0_attn_b_weight_qkv': _L0_attn_b_in['weight_qkv'], 'L0_attn_b_weight_out': _L0_attn_b_in['weight_out'], 'L0_ffn_SU_ug': _L0_ffn_in['SU_ug'], 'L0_ffn_SU_dp': _L0_ffn_in['SU_dp'], 'L0_ffn_Wscale_ug': _L0_ffn_in['Wscale_ug'], 'L0_ffn_Wscale_dp': _L0_ffn_in['Wscale_dp'], 'L0_ffn_W_up': _L0_ffn_in['W_up'], 'L0_ffn_W_gate': _L0_ffn_in['W_gate'], 'L0_ffn_W_down': _L0_ffn_in['W_down']}
    _x0 = _d['L0_attn_a_x']
    _d['L0_attn_a_x'] = jax.random.normal(jax.random.fold_in(jax.random.key(seed), 1), (1, 2048, 256), dtype=_x0.dtype)
    del _x0
    return _d

def reference(L0_attn_a_x, L0_attn_a_w_q, L0_attn_a_w_k, L0_attn_a_w_v, L0_attn_a_w_o, L0_attn_b_weight_qkv, L0_attn_b_weight_out, L0_ffn_SU_ug, L0_ffn_SU_dp, L0_ffn_Wscale_ug, L0_ffn_Wscale_dp, L0_ffn_W_up, L0_ffn_W_gate, L0_ffn_W_down):

    def _L0_attn_a_ref(x, w_q, w_k, w_v, w_o):
        import jax, jax.numpy as jnp
        import numpy as np
        D_MODEL = 256
        NUM_HEADS = 16
        D_HEAD = D_MODEL // NUM_HEADS
        b, s, _ = x.shape

        def split_heads(t):
            return t.reshape(b, s, NUM_HEADS, D_HEAD).transpose(0, 2, 1, 3)
        q = split_heads(x @ w_q)
        k = split_heads(x @ w_k)
        v = split_heads(x @ w_v)
        scale = 1.0 / np.sqrt(D_HEAD).astype(np.float32)
        scores = jnp.einsum('bhqd,bhkd->bhqk', q, k) * scale
        causal = jnp.tril(jnp.ones((s, s), dtype=bool))
        scores = jnp.where(causal, scores, -jnp.inf)
        probs = jax.nn.softmax(scores, axis=-1)
        attn = jnp.einsum('bhqk,bhkd->bhqd', probs, v)
        attn = attn.transpose(0, 2, 1, 3).reshape(b, s, D_MODEL)
        return attn @ w_o

    def _L0_attn_b_ref(x, weight_qkv, weight_out):
        import jax, jax.numpy as jnp
        import numpy as np
        L, N, E, H = (256, 2, 256, 16)
        DH = E // H
        SCALE = DH ** (-0.5)
        l, n, e = x.shape
        h, dh = (H, DH)
        qkv = jnp.einsum('lne,fe->lnf', x, weight_qkv)
        q, k, v = jnp.split(qkv, 3, axis=-1)
        q = q.reshape(l, n, h, dh) * jnp.asarray(SCALE, x.dtype)
        k = k.reshape(l, n, h, dh)
        v = v.reshape(l, n, h, dh)
        attn = jnp.einsum('lnhd,mnhd->nhlm', q, k)
        causal = jnp.tril(jnp.ones((l, l), dtype=bool))
        attn = jnp.where(causal, attn, jnp.asarray(-jnp.inf, attn.dtype))
        attn = jax.nn.softmax(attn, axis=-1)
        out = jnp.einsum('nhlm,mnhd->lnhd', attn, v).reshape(l, n, e)
        return jnp.einsum('lne,fe->lnf', out, weight_out)

    def _L0_ffn_ref(input, SU_ug, SU_dp, Wscale_ug, Wscale_dp, W_up, W_gate, W_down):
        import jax, jax.numpy as jnp
        import numpy as np
        HIDDEN = 256
        INTER = 1024
        SCALE = 64.0

        def fwht(x):
            orig_shape = x.shape
            n = orig_shape[-1]
            x = x.reshape(-1, n)
            h = 1
            while h < n:
                x = x.reshape(-1, n // (2 * h), 2, h)
                a, b = (x[:, :, 0, :], x[:, :, 1, :])
                x = jnp.stack([a + b, a - b], axis=2).reshape(-1, n)
                h *= 2
            return (x / jnp.sqrt(jnp.asarray(n, x.dtype))).reshape(orig_shape)
        n = SU_ug.shape[0]
        x = input.reshape(-1, n)
        x = fwht(x * SU_ug) / SCALE
        x_up = x @ W_up.T * (Wscale_ug[:INTER] * SCALE)
        x_gate = x @ W_gate.T * (Wscale_ug[INTER:] * SCALE)
        x = jax.nn.silu(x_gate) * x_up
        x = fwht(x * SU_dp) / SCALE
        x = x @ W_down.T * (Wscale_dp * SCALE)
        return x.reshape(input.shape)
    x = L0_attn_a_x
    x = x + _L0_attn_a_ref(_layernorm(x, axis=-1), L0_attn_a_w_q, L0_attn_a_w_k, L0_attn_a_w_v, L0_attn_a_w_o)
    x = x + _L0_ffn_ref(_layernorm(x, axis=-1), L0_ffn_SU_ug, L0_ffn_SU_dp, L0_ffn_Wscale_ug, L0_ffn_Wscale_dp, L0_ffn_W_up, L0_ffn_W_gate, L0_ffn_W_down)
    x = x + _L0_attn_b_ref(_layernorm(x, axis=-1), L0_attn_b_weight_qkv, L0_attn_b_weight_out)
    x = x + _L0_ffn_ref(_layernorm(x, axis=-1), L0_ffn_SU_ug, L0_ffn_SU_dp, L0_ffn_Wscale_ug, L0_ffn_Wscale_dp, L0_ffn_W_up, L0_ffn_W_gate, L0_ffn_W_down)
    return x

_drawn_inputs = setup_inputs


def setup_inputs(seed=0):
    import zlib

    import numpy as np

    out = dict(_drawn_inputs(seed))
    spreads = {}
    factors = {'L0_ffn_Wscale_dp': 2.795}
    for name, (base, spread) in spreads.items():
        noise = np.random.default_rng([zlib.crc32(name.encode()), seed]).standard_normal(out[name].shape)
        drawn = base * np.exp(spread * noise) if base else spread * noise
        out[name] = jnp.asarray(drawn.astype(out[name].dtype))
    for name, factor in factors.items():
        out[name] = (out[name] * factor).astype(out[name].dtype)
    return out
```

```python
import concourse.bass as bass
from concourse import mybir
from contextlib import ExitStack

fp32 = mybir.dt.float32
fp32r = mybir.dt.float32r
bf16 = mybir.dt.bfloat16
ALU = mybir.AluOpType
ACT = mybir.ActivationFunctionType
AX = mybir.AxisListType

P = 128
S = 2048
D = 256
KD = D // P
HEADS = 16
DH = D // HEADS
INTER = 1024
KF = INTER // P
CH = 512
NCH = S // CH
TPC = CH // P
TILES = S // P
GH = 4
NG = HEADS // GH
FFN_SCALE = 64.0
EPS = 1e-5
MASKED = -3.0e38
Q_PARTS = (0, 0, 1, 1, 0, 2)
K_PARTS = (0, 1, 0, 1, 2, 0)
KS = len(Q_PARTS) * DH
KM = KS + 2
VW = DH + 1
PASSES = ((0, 0), (0, 1), (1, 0))


def clear(nc, sems):
    nc.all_engine_barrier()
    for s in sems:
        nc.gpsimd.sem_clear(s)
    nc.all_engine_barrier()


def build_constants(nc, ident, identb, causal, spread, hadamard, tmp, ones, rootexp):
    with ExitStack() as ctx:
        filled = ctx.enter_context(nc.semaphore("c_filled"))
        ready = ctx.enter_context(nc.semaphore("c_ready"))
        level = ctx.enter_context(nc.semaphore("c_level"))
        with nc.Block() as block:
            @block.gpsimd
            def _(pool):
                nc.gpsimd.memset(ident[:], 0.0).then_inc(filled, 1)
                nc.gpsimd.memset(identb[:], 0.0).then_inc(filled, 1)
                nc.gpsimd.memset(causal[:], 0.0).then_inc(filled, 1)
                nc.gpsimd.memset(spread[:], 0.0).then_inc(filled, 1)
                nc.gpsimd.memset(ones[:], 1.0).then_inc(filled, 1)
                nc.gpsimd.memset(rootexp[:], -0.5).then_inc(filled, 1)
                pool.wait_ge(filled, 6)
                nc.gpsimd.affine_select(out=ident[:], in_=ident[:], compare_op=ALU.not_equal, fill=1.0, base=0,
                                        pattern=[[-1, P]], channel_multiplier=1).then_inc(ready, 1)
                nc.gpsimd.affine_select(out=identb[:], in_=identb[:], compare_op=ALU.not_equal, fill=1.0, base=0,
                                        pattern=[[-1, P]], channel_multiplier=1).then_inc(ready, 1)
                nc.gpsimd.affine_select(out=causal[:], in_=causal[:], compare_op=ALU.is_ge, fill=MASKED, base=0,
                                        pattern=[[-1, P]], channel_multiplier=1).then_inc(ready, 1)
                nc.gpsimd.affine_select(out=spread[:].rearrange("p (j c) -> p j c", j=GH),
                                        in_=spread[:].rearrange("p (j c) -> p j c", j=GH),
                                        compare_op=ALU.not_equal, fill=1.0, base=-DH,
                                        pattern=[[-32, GH], [0, 32]], channel_multiplier=1).then_inc(ready, 1)

            @block.vector
            def _(dve):
                dve.wait_ge(ready, 1)
                src, n, width = ident, 0, 1
                while width < P:
                    dst = hadamard if src is not hadamard else tmp
                    a = src[:].rearrange("p (a two h) -> p a two h", two=2, h=width)
                    b = dst[:].rearrange("p (a two h) -> p a two h", two=2, h=width)
                    if n:
                        dve.wait_ge(level, n)
                    nc.vector.tensor_tensor(b[:, :, 0, :], a[:, :, 0, :], a[:, :, 1, :], ALU.add).then_inc(level, 1)
                    nc.vector.tensor_tensor(b[:, :, 1, :], a[:, :, 0, :], a[:, :, 1, :], ALU.subtract).then_inc(level, 1)
                    src, n, width = dst, n + 2, 2 * width
                assert src is hadamard
        clear(nc, (filled, ready, level))


def build_projections(nc, x, w_q, w_k, w_v, ident, rootexp, ones, qs, ks, v_aug, o_all):
    NU = 2 * KD
    UNITS = NU + TPC // 2
    lent = o_all[:].rearrange("p g s -> p (g s)")
    SLOTS = 6
    parts = lent[:, 0:SLOTS * 3 * CH // 2].bitcast(bf16).rearrange("p (u a n) -> p u a n", u=SLOTS, a=3)
    at = SLOTS * 3 * CH // 2
    wraw = lent[:, at:at + 3 * KD * D].rearrange("p (w k n) -> p w k n", w=3, k=KD)
    at += 3 * KD * D
    rest = lent[:, at:at + 2 * CH].rearrange("p (u n) -> p u n", u=2)
    scratch = nc.dram_tensor("qk_parts", (2, 3, D, S), bf16).ap()
    with ExitStack() as ctx:
        def sb(name, shape, dt=fp32):
            return ctx.enter_context(nc.sbuf_tensor(name, shape, dt))

        xin = sb("xin", [P, 2, TPC, D])
        xT = [sb(f"xT{i}", [P, KD, CH], fp32r) for i in range(2)]
        wsp = [sb(f"wsp{i}", [P, 3, KD, D], fp32r) for i in range(2)]
        stats = sb("stats1", [P, TPC, 6])
        mv = sb("mv1", [P, TPC, 2])
        rstd = sb("rstd1", [P, TPC, 2])
        psT = ctx.enter_context(nc.psum_tensor("psT1", [P, KD, CH], fp32))
        unit = [ctx.enter_context(nc.psum_tensor(f"unit{i}", [P, CH], fp32)) for i in range(UNITS)]

        names = ["x_in0", "x_in1", "w_in", "w_high", "w_low", "stats_done", "aggregated", "eps_added", "rstd_done",
                 "normed", "transposed", "high_done", "low_done", "unit_done", "part1_done", "rest_done",
                 "part2_done", "parts_done", "v_done", "ones_in", "v_ones", "stacked"]
        sems = {n: ctx.enter_context(nc.semaphore("p_" + n)) for n in names}
        stored = [ctx.enter_context(nc.semaphore(f"p_stored{i}")) for i in range(SLOTS)]
        x_in = (sems["x_in0"], sems["x_in1"])
        g = sems
        with nc.Block() as block:
            @block.sync
            def _(sp):
                for n, w in enumerate((w_q, w_k, w_v)):
                    sp.dma_start(wraw[:, n, :, :], w.rearrange("(k p) n -> p k n", p=P)).then_inc(g["w_in"], 16)
                for r in range(2):
                    sp.dma_start(ks[KS + r:KS + r + 1, :, :].rearrange("p h (b n) -> p (h b) n", n=CH),
                                 ones[64 * r:64 * r + 64, :]).then_inc(g["ones_in"], 16)
                for n in range(NU * NCH + 2):
                    if n < NU * NCH:
                        c, u = divmod(n, NU)
                        sp.wait_ge(g["parts_done"], n + 1)
                        sp.dma_start(scratch[u // KD, :, P * (u % KD):P * (u % KD) + P, CH * c:CH * c + CH].rearrange("a p n -> p a n"),
                                     parts[:, n % SLOTS, :, :]).then_inc(stored[n % SLOTS], 16)
                    if n >= 2:
                        m = n - 2
                        c, u = divmod(m, NU)
                        stack, order = (qs, Q_PARTS) if u < KD else (ks, K_PARTS)
                        sp.wait_ge(stored[m % SLOTS], 16 * (m // SLOTS + 1))
                        for t, part in enumerate(order):
                            h0 = P // DH * (u % KD)
                            sp.dma_start(
                                stack[DH * t:DH * t + DH, h0:h0 + P // DH, CH * c:CH * c + CH],
                                scratch[u // KD, part, P * (u % KD):P * (u % KD) + P, CH * c:CH * c + CH]
                                .rearrange("(h d) n -> d h n", d=DH)).then_inc(g["stacked"], 16)
                sp.wait_ge(g["stacked"], 16 * len(Q_PARTS) * NU * NCH)
                sp.wait_ge(g["ones_in"], 32)

            def chunk(act, c):
                act.wait_ge(g["transposed"], c + 1)
                if c:
                    act.wait_ge(g["unit_done"], UNITS * c)
                nc.scalar.copy(xT[0][:], psT[:]).then_inc(g["high_done"], 1)
                for u in range(UNITS):
                    act.wait_ge(g["unit_done"], UNITS * c + u + 1)
                    if u < NU:
                        n = NU * c + u
                        if n >= SLOTS:
                            act.wait_ge(stored[n % SLOTS], 16 * (n // SLOTS))
                        nc.scalar.copy(parts[:, n % SLOTS, 0, :], unit[u][:]).then_inc(g["part1_done"], 1)
                    else:
                        if c == 0:
                            act.wait_ge(g["v_ones"], 1)
                        t = TPC * c + 2 * (u - NU)
                        nc.scalar.copy(v_aug[:, t:t + 2, :, 0:DH],
                                       unit[u][:].rearrange("p (t h d) -> p t h d", t=2, d=DH)).then_inc(g["v_done"], 1)

            @block.scalar
            def _(act):
                for c in range(NCH):
                    if c >= 2:
                        act.wait_ge(g["transposed"], c - 1)
                    act.dma_start(xin[:, c % 2, :, :],
                                  x[0, CH * c:CH * c + CH, :].rearrange("(t p) d -> p t d", p=P)).then_inc(x_in[c % 2], 16)
                    if c == 0:
                        continue
                    chunk(act, c - 1)
                chunk(act, NCH - 1)

            @block.gpsimd
            def _(pool):
                nc.gpsimd.memset(v_aug[:, :, :, DH:VW], 1.0).then_inc(g["v_ones"], 1)

                def root(c):
                    pool.wait_ge(g["aggregated"], TPC * (c + 1))
                    nc.gpsimd.tensor_scalar(rstd[:, :, 0], mv[:, :, 1], EPS, None, ALU.add).then_inc(g["eps_added"], 1)
                    pool.wait_ge(g["eps_added"], c + 1)
                    nc.gpsimd.tensor_tensor(rstd[:, :, 1], rstd[:, :, 0], rootexp[:], ALU.pow).then_inc(g["rstd_done"], 1)

                root(0)
                for c in range(NCH):
                    if c + 1 < NCH:
                        root(c + 1)
                    for u in range(NU):
                        n = NU * c + u
                        slot = n % SLOTS
                        pool.wait_ge(g["rest_done"], n + 1)
                        nc.gpsimd.tensor_copy(parts[:, slot, 1, :], rest[:, n % 2, :]).then_inc(g["part2_done"], 1)
                        pool.wait_ge(g["part2_done"], n + 1)
                        nc.gpsimd.tensor_tensor(parts[:, slot, 2, :], rest[:, n % 2, :], parts[:, slot, 1, :],
                                                ALU.subtract).then_inc(g["parts_done"], 1)

            @block.vector
            def _(dve):
                def statistics(c):
                    dve.wait_ge(x_in[c % 2], 16 * (c // 2 + 1))
                    if c:
                        dve.wait_ge(g["normed"], TPC * c)
                    for t in range(TPC):
                        nc.vector.bn_stats(stats[:, t, :], xin[:, c % 2, t, :]).then_inc(g["stats_done"], 1)
                    for t in range(TPC):
                        dve.wait_ge(g["stats_done"], TPC * c + t + 1)
                        nc.vector.bn_aggr(mv[:, t, :], stats[:, t, :]).then_inc(g["aggregated"], 1)

                def normalise(c):
                    dve.wait_ge(g["rstd_done"], c + 1)
                    for t in range(TPC):
                        nc.vector.tensor_scalar(xin[:, c % 2, t, :], xin[:, c % 2, t, :], mv[:, t, 0:1],
                                                rstd[:, t, 1:2], ALU.subtract, ALU.mult).then_inc(g["normed"], 1)

                statistics(0)
                normalise(0)
                dve.wait_ge(g["w_in"], 48)
                nc.vector.tensor_copy(wsp[0][:], wraw[:]).then_inc(g["w_high"], 1)
                dve.wait_ge(g["w_high"], 1)
                nc.vector.tensor_tensor(wsp[1][:], wraw[:], wsp[0][:].bitcast(fp32), ALU.subtract).then_inc(g["w_low"], 1)
                for c in range(NCH):
                    dve.wait_ge(g["high_done"], c + 1)
                    nc.vector.tensor_tensor(xT[1][:], psT[:], xT[0][:].bitcast(fp32), ALU.subtract).then_inc(g["low_done"], 1)
                    if c + 1 < NCH:
                        statistics(c + 1)
                    for u in range(NU):
                        n = NU * c + u
                        dve.wait_ge(g["part1_done"], n + 1)
                        if n >= 2:
                            dve.wait_ge(g["parts_done"], n - 1)
                        nc.vector.tensor_tensor(rest[:, n % 2, :], unit[u][:], parts[:, n % SLOTS, 0, :],
                                                ALU.subtract).then_inc(g["rest_done"], 1)
                    if c + 1 < NCH:
                        normalise(c + 1)

            @block.tensor
            def _(pe):
                def transposes(c):
                    pe.wait_ge(g["normed"], TPC * (c + 1))
                    if c:
                        pe.wait_ge(g["low_done"], c)
                    for k in range(KD):
                        for t in range(TPC):
                            last = nc.tensor.transpose(psT[:, k, P * t:P * t + P], xin[:, c % 2, t, P * k:P * k + P], ident[:])
                    last.then_inc(g["transposed"], 1)

                transposes(0)
                pe.wait_ge(g["w_low"], 1)
                for c in range(NCH):
                    pe.wait_ge(g["low_done"], c + 1)
                    for u in range(UNITS):
                        if c and u < NU:
                            pe.wait_ge(g["rest_done"], NU * (c - 1) + u + 1)
                        if c and u >= NU:
                            pe.wait_ge(g["v_done"], (UNITS - NU) * (c - 1) + u - NU + 1)
                        steps = [(k, a, b) for k in range(KD) for a, b in PASSES]
                        if u < NU:
                            m = u % KD
                            for i, (k, a, b) in enumerate(steps):
                                last = nc.tensor.matmul(unit[u][:], wsp[a][:, u // KD, k, P * m:P * m + P], xT[b][:, k, :],
                                                        start=(i == 0), stop=(i == len(steps) - 1))
                        else:
                            for t in range(2):
                                at = P * (2 * (u - NU) + t)
                                for i, (k, a, b) in enumerate(steps):
                                    last = nc.tensor.matmul(unit[u][:, D * t:D * t + D], xT[a][:, k, at:at + P], wsp[b][:, 2, k, :],
                                                            start=(i == 0), stop=(i == len(steps) - 1))
                        last.then_inc(g["unit_done"], 1)
                    if c + 1 < NCH:
                        transposes(c + 1)
        clear(nc, [*sems.values(), *stored])


def max_pieces(item):
    step, c = item
    out = []
    for qb in range(TPC * c, TPC * c + TPC):
        n = P * (qb + 1)
        if n <= CH:
            for j in (0, 2):
                out.append((step, c, qb, ((j, 0, n), (j + 1, 0, n)), 0))
        else:
            for j in range(GH):
                for s, k0 in enumerate(range(0, n, 2 * CH)):
                    banks = tuple((j, a, min(CH, n - a)) for a in range(k0, min(n, k0 + 2 * CH), CH))
                    out.append((step, c, qb, banks, s))
    return out


def score_quads(c):
    return [(c, kb, P * max(0, kb - TPC * c), CH - P * max(0, kb - TPC * c)) for kb in range(TPC * (c + 1))]


def plan(score_chunks, max_items):
    quads = [q for c in score_chunks for q in score_quads(c)]
    work = []
    npiece = 0
    for n, item in enumerate(max_items):
        for m, p in enumerate(max_pieces(item)):
            if n and m == 3:
                work.append(("T", n - 1, 0))
            work.append(("M", npiece, sum(b[2] for b in p[3])))
            npiece += 1
    if max_items:
        work.append(("T", len(max_items) - 1, 3 * CH))
    order, done, seen = [], 0, 0
    work.reverse()
    pending_norm = None
    for n, (c, kb, q0, nq) in enumerate(quads):
        for j in range(GH):
            order.append(("S", n, j))
            seen += nq
            while work and done + (work[-1][2] if work[-1][0] == "T" else 0) < seen:
                kind, k, cols = work.pop()
                order.append((kind, k))
                done += cols
        if n:
            order.append(("V", n - 1))
            if pending_norm is not None:
                order.append(("R", pending_norm))
                pending_norm = None
            if quads[n - 1][0] != c:
                pending_norm = quads[n - 1][0]
    while work:
        kind, k, _ = work.pop()
        order.append((kind, k))
    if quads:
        if pending_norm is not None:
            order.append(("R", pending_norm))
        order.append(("V", len(quads) - 1))
        order.append(("R", quads[-1][0]))
    return quads, order


ST_BANKS = 3
P_SLOTS = 8
ROWS_IN = 16 * 2 * GH


def build_attention_step(nc, group, score_chunks, max_items, t):
    quads, order = plan(score_chunks, max_items)
    pieces = [p for item in max_items for p in max_pieces(item)]
    qs, ks, v_aug, v_group, o_all = t["qs"], t["ks"], t["v_aug"], t["v_group"], t["o_all"]
    mx, mparts, mrow, mtmp = t["mx"], t["mparts"], t["mrow"], t["mtmp"]
    probs, oraw, rec = t["probs"], t["oraw"], t["rec"]
    smax, st, ops = t["smax"], t["st"], t["ops"]
    g = t["sems"]
    smax_uses = [o for o in order if o[0] in "MT"]
    st_uses = [o for o in order if o[0] in "SR"]
    smax_at = {o: n for n, o in enumerate(smax_uses)}
    st_at = {o: n for n, o in enumerate(st_uses)}
    act_frees, dve_frees, frees = 0, 0, []
    for o in st_uses:
        if o[0] == "S":
            act_frees += 1
            frees.append(("exp_done", act_frees))
        else:
            dve_frees += 1
            frees.append(("reciprocal_done", dve_frees))
    diag = [q[1] >= TPC * q[0] for q in quads]
    masks_before = [GH * sum(diag[:n]) for n in range(len(quads) + 1)]
    chunk_no = {c: n for n, c in enumerate(score_chunks)}
    chunk_last = {c: max(n for n, q in enumerate(quads) if q[0] == c) for c in score_chunks}

    with nc.Block(no_gpsimd_drain=True) as block:
        @block.tensor
        def _(pe):
            for o in order:
                if o[0] in "MT":
                    n = smax_at[o]
                    if n >= 2:
                        pe.wait_ge(g["smax_read"], n - 1)
                    if o[0] == "M":
                        step, c, qb, banks, _ = pieces[o[1]]
                        for b, (j, k0, nk) in enumerate(banks):
                            head = GH * (group + step) + j
                            masked = k0 + nk == P * (qb + 1)
                            last = nc.tensor.matmul(smax[n % 2][:, CH * b:CH * b + nk],
                                                    qs[0:KS, head, P * qb:P * qb + P], ks[0:KS, head, k0:k0 + nk],
                                                    start=True, stop=not masked)
                            if masked:
                                last = nc.tensor.matmul(smax[n % 2][:, CH * b + nk - P:CH * b + nk], t["identb"][:], t["causal"][:],
                                                        start=False, stop=True)
                    else:
                        pe.wait_ge(g["mparts_done"], o[1] + 1)
                        last = nc.tensor.transpose(smax[n % 2][0:32, 0:P // 2].bitcast(bf16), mparts[:], t["identb"][:])
                    last.then_inc(g["smax_done"], 1)
                elif o[0] == "S":
                    _, n, j = o
                    c, kb, q0, nq = quads[n]
                    use = st_at[o]
                    if use >= ST_BANKS:
                        pe.wait_ge(g[frees[use - ST_BANKS][0]], frees[use - ST_BANKS][1])
                    if j == 0 and kb == 0 and (0, c) in max_items:
                        pe.wait_ge(g["max_row"], ROWS_IN * (max_items.index((0, c)) + 1))
                    head = GH * group + j
                    nc.tensor.matmul(st[use % ST_BANKS][:, 0:nq], ks[0:KM, head, P * kb:P * kb + P],
                                     qs[0:KM, head, CH * c + q0:CH * c + CH], start=True, stop=True).then_inc(g["score_done"], 1)
                elif o[0] == "V":
                    n = o[1]
                    c, kb, q0, nq = quads[n]
                    if n == 0:
                        pe.wait_ge(g["v_group_done"], 1)
                    if kb == 0 and chunk_no[c]:
                        pe.wait_ge(g["o_read"], chunk_no[c])
                    for j in range(GH):
                        u = GH * n + j
                        pe.wait_ge(g["exp_done"], u + 1)
                        if diag[n]:
                            pe.wait_ge(g["masked"], masks_before[n] + j + 1)
                        nc.tensor.matmul(ops[32 * j:32 * j + VW, q0:CH], v_group[:, kb, j, :], probs[:, u % P_SLOTS, 0:nq],
                                         start=(kb == 0), stop=(kb == TPC * (c + 1) - 1)).then_inc(g["pv_done"], 1)
                else:
                    c = o[1]
                    use = st_at[o]
                    if use >= ST_BANKS:
                        pe.wait_ge(g[frees[use - ST_BANKS][0]], frees[use - ST_BANKS][1])
                    pe.wait_ge(g["o_read"], chunk_no[c] + 1)
                    nc.tensor.matmul(st[use % ST_BANKS][:], t["spread"][:], oraw[:, chunk_no[c] % 2, :], start=True, stop=True)\
                        .then_inc(g["sums_spread"], 1)

        def evacuate(act, c):
            act.wait_ge(g["pv_done"], GH * (chunk_last[c] + 1))
            n = chunk_no[c]
            if n >= 2:
                act.wait_ge(g["o_scaled"], n - 1)
            nc.scalar.copy(oraw[:, n % 2, :], ops[:]).then_inc(g["o_read"], 1)

        @block.scalar
        def _(act):
            for n, (c, kb, q0, nq) in enumerate(quads):
                for j in range(GH):
                    u = GH * n + j
                    act.wait_ge(g["score_done"], u + 1)
                    if u >= P_SLOTS:
                        act.wait_ge(g["pv_done"], u - P_SLOTS + 1)
                    nc.scalar.activation(probs[:, u % P_SLOTS, 0:nq], st[st_at[("S", n, j)] % ST_BANKS][:, 0:nq], ACT.Exp,
                                         scale=DH ** -0.5).then_inc(g["exp_done"], 1)
                if kb == 0 and chunk_no[c]:
                    evacuate(act, score_chunks[chunk_no[c] - 1])
            if quads:
                evacuate(act, score_chunks[-1])

        @block.vector
        def _(dve):
            pending = list(order)
            piece_end = {}
            at = 0
            for n, item in enumerate(max_items):
                at += len(max_pieces(item))
                piece_end[n] = at
            if quads:
                nc.vector.tensor_copy(v_group[:], v_aug[:, :, bass.ds(GH * group, GH), :] if not isinstance(group, int)
                                      else v_aug[:, :, GH * group:GH * group + GH, :]).then_inc(g["v_group_done"], 1)
            reads = 0
            combined = 0
            for o in pending:
                if o[0] == "M":
                    step, c, qb, banks, s = pieces[o[1]]
                    if o[1] in piece_end.values():
                        dve.wait_ge(g["mparts_done"], [k for k, v in piece_end.items() if v == o[1]][0] + 1)
                    n = smax_at[o]
                    dve.wait_ge(g["smax_done"], n + 1)
                    buf = smax[n % 2]
                    if len(banks) == 2 and banks[0][0] != banks[1][0]:
                        j, nk = banks[0][0], banks[0][2]
                        src = buf[:].rearrange("p (b n) -> p b n", b=2)[:, :, 0:nk]
                        dst = mx[:, j:j + 2, qb % TPC, s]
                    else:
                        src = buf[:, 0:sum(b[2] for b in banks)]
                        dst = mx[:, banks[0][0], qb % TPC, s:s + 1]
                    nc.vector.reduce_max(dst, src, AX.X).then_inc(g["smax_read"], 1)
                    reads += 1
                    if o[1] + 1 in piece_end.values():
                        n = [k for k, v in piece_end.items() if v == o[1] + 1][0]
                        dve.wait_ge(g["smax_read"], reads)
                        high = mparts[:, 0:GH * TPC].rearrange("p (j q) -> p j q", j=GH)
                        low = mparts[:, GH * TPC:2 * GH * TPC].rearrange("p (j q) -> p j q", j=GH)
                        if c >= 2:
                            nc.vector.tensor_tensor(mtmp[:], mx[:, :, :, 0], mx[:, :, :, 1], ALU.max).then_inc(g["combined"], 1)
                            combined += 1
                            dve.wait_ge(g["combined"], combined)
                            m = mtmp[:]
                        else:
                            m = mx[:, :, :, 0]
                        nc.vector.tensor_scalar(high, m, -1.0, None, ALU.mult).then_inc(g["combined"], 1)
                        combined += 1
                        dve.wait_ge(g["combined"], combined)
                        nc.vector.scalar_tensor_tensor(out=low, in0=m, scalar=-1.0, in1=high, op0=ALU.mult,
                                                       op1=ALU.subtract).then_inc(g["mparts_done"], 1)
                elif o[0] == "T":
                    n = smax_at[o]
                    dve.wait_ge(g["smax_done"], n + 1)
                    if o[1]:
                        dve.wait_ge(g["max_row"], ROWS_IN * o[1])
                    nc.vector.tensor_copy(mrow[:], smax[n % 2][0:32, 0:P // 2].bitcast(bf16)).then_inc(g["smax_read"], 1)
                    reads += 1
                elif o[0] == "R":
                    c = o[1]
                    n = chunk_no[c]
                    dve.wait_ge(g["sums_spread"], n + 1)
                    if n:
                        dve.wait_ge(g["o_scaled"], n)
                    nc.vector.reciprocal(rec[:], st[st_at[o] % ST_BANKS][:]).then_inc(g["reciprocal_done"], 1)

        @block.gpsimd
        def _(pool):
            scaled = 0

            def scale(c):
                n = chunk_no[c]
                pool.wait_ge(g["reciprocal_done"], n + 1)
                dst = o_all[:, group, CH * c:CH * c + CH]
                nc.gpsimd.tensor_tensor(dst, oraw[:, n % 2, :], rec[:], ALU.mult).then_inc(g["o_scaled"], 1)

            for n, (c, kb, q0, nq) in enumerate(quads):
                if diag[n]:
                    if kb == TPC * c and chunk_no[c] and c >= 1:
                        scale(score_chunks[chunk_no[c] - 1])
                        scaled += 1
                    for j in range(GH):
                        u = GH * n + j
                        pool.wait_ge(g["exp_done"], u + 1)
                        blk = probs[:, u % P_SLOTS, 0:P]
                        nc.gpsimd.affine_select(out=blk, in_=blk, compare_op=ALU.is_ge, fill=0.0, base=0,
                                                pattern=[[1, P]], channel_multiplier=-1).then_inc(g["masked"], 1)
            for c in score_chunks[scaled:]:
                scale(c)

        @block.sync
        def _(sp):
            for n, (step, c) in enumerate(max_items):
                sp.wait_ge(g["smax_read"], smax_at[("T", n)] + 1)
                for r in range(2):
                    for j in range(GH):
                        row = GH * TPC * r + TPC * j
                        dst = qs[KS + r:KS + r + 1, GH * (group + step) + j, CH * c:CH * c + CH]
                        sp.dma_start(dst.rearrange("p (b q) -> p b q", q=P), mrow[row:row + TPC, :])\
                            .then_inc(g["max_row"], 16)
            if max_items:
                sp.wait_ge(g["max_row"], ROWS_IN * len(max_items))
    clear(nc, list(g.values()))


def build_attention(nc, ctx, t, loop):
    def sb(name, shape, dt=fp32):
        return ctx.enter_context(nc.sbuf_tensor(name, shape, dt))

    t = dict(t)
    t["v_group"] = sb("v_group", [P, TILES, GH, VW])
    t["mx"] = sb("mx", [P, GH, TPC, 2])
    t["mtmp"] = sb("mtmp", [P, GH, TPC])
    t["mparts"] = sb("mparts", [P, 2 * GH * TPC], bf16)
    t["mrow"] = sb("mrow", [32, P], bf16)
    t["probs"] = sb("probs", [P, P_SLOTS, CH])
    t["oraw"] = sb("oraw", [P, 2, CH])
    t["rec"] = sb("rec", [P, CH])
    t["smax"] = [ctx.enter_context(nc.psum_tensor(f"smax{i}", [P, 2 * CH], fp32)) for i in range(2)]
    t["st"] = [ctx.enter_context(nc.psum_tensor(f"st{i}", [P, CH], fp32)) for i in range(ST_BANKS)]
    t["ops"] = ctx.enter_context(nc.psum_tensor("ops", [P, CH], fp32))
    names = ["smax_done", "smax_read", "mparts_done", "max_row", "score_done", "exp_done", "masked", "pv_done", "o_read",
             "sums_spread", "reciprocal_done", "o_scaled", "v_group_done", "combined", "zeroed", "ops_zeroed"]
    t["sems"] = {n: ctx.enter_context(nc.semaphore("a_" + n)) for n in names}
    g = t["sems"]

    with nc.Block() as block:
        @block.vector
        def _(dve):
            nc.vector.memset(t["probs"][:, 0, :], 0.0).then_inc(g["zeroed"], 1)

        @block.tensor
        def _(pe):
            pe.wait_ge(g["zeroed"], 1)
            nc.tensor.matmul(t["ops"][:], t["probs"][:, 0, 0:P], t["probs"][:, 0, :], start=True, stop=True)\
                .then_inc(g["ops_zeroed"], 1)
    clear(nc, [g["zeroed"], g["ops_zeroed"]])

    chunks = list(range(NCH))
    build_attention_step(nc, 0, [], [(0, c) for c in chunks[:-1]], t)
    items = [(0, NCH - 1)] + [(1, c) for c in chunks[:-1]]
    if loop:
        with nc.Fori(0, NG - 1) as group:
            build_attention_step(nc, group, chunks, items, t)
    else:
        for group in range(NG - 1):
            build_attention_step(nc, group, chunks, items, t)
    build_attention_step(nc, NG - 1, chunks, [(0, NCH - 1)], t)


def build_weights(nc, ins, c, w):
    with ExitStack() as ctx:
        def sb(name, shape, dt=fp32):
            return ctx.enter_context(nc.sbuf_tensor(name, shape, dt))

        up = sb("up_raw", [P, 2 * KF, D])
        upT = sb("upT", [P, KD, 2 * INTER])
        down = sb("down_raw", [P, KD, INTER])
        downT = sb("downT", [P, KF, D])
        fly = [sb(f"fly{i}", [P, KF, D]) for i in range(2)]
        wv = sb("wv_raw", [P, KD, D])
        wout = sb("wout_raw", [P, KD, D])
        woutT = sb("woutT", [P, KD, D])
        negh = sb("negh", [P, P])
        su = sb("su", [P, KD])
        sud = sb("sud", [P, KF])
        sud32 = sb("sud32", [P, KF])
        sdp = sb("sdp", [P, D])
        full = sb("full", [P, 2, CH])
        ps = [ctx.enter_context(nc.psum_tensor(f"wps{i}", [P, CH], fp32)) for i in range(8)]
        names = ["in_up", "in_down", "in_attn", "in_small", "in_wo", "zero", "neg", "pe_done", "dve_copy", "full", "high", "low"]
        g = {n: ctx.enter_context(nc.semaphore("w_" + n)) for n in names}
        jobs = [("tu", f, k) for k in range(KD) for f in range(0, 2 * KF, 4)]
        jobs += [("td", gt, 0) for gt in range(0, KF, 2)]
        jobs += [("to", 0, 0)]
        jobs += [("hu", a, f) for a in range(KD) for f in range(2 * INTER // CH)]
        jobs += [("hd", b, 0) for b in range(0, KF, 2)]
        jobs += [("ab", 0, 0)]
        need = {"hu": sum(j[0] == "tu" for j in jobs)}
        need["hd"] = need["hu"] + sum(j[0] == "td" for j in jobs)
        need["ab"] = need["hd"] + 1
        plain = [j[0] not in ("hu", "ab") for j in jobs]
        copied = [sum(plain[:n + 1]) for n in range(len(jobs))]
        with nc.Block() as block:
            @block.sync
            def _(sp):
                sp.dma_start(up[:, 0:KF, :], ins["W_up"].rearrange("(f p) j -> p f j", p=P)).then_inc(g["in_up"], 16)
                sp.dma_start(up[:, KF:2 * KF, :], ins["W_gate"].rearrange("(f p) j -> p f j", p=P)).then_inc(g["in_up"], 16)
                sp.dma_start(down[:], ins["W_down"].rearrange("(k p) j -> p k j", p=P)).then_inc(g["in_down"], 16)
                sp.dma_start(wv[:], ins["weight_qkv"][2 * D:3 * D, :].rearrange("(k p) j -> p k j", p=P)).then_inc(g["in_attn"], 16)
                sp.dma_start(wout[:], ins["weight_out"].rearrange("(k p) j -> p k j", p=P)).then_inc(g["in_attn"], 16)
                sp.dma_start(w["resid"][:], ins["x"][0].rearrange("(t p) d -> p t d", p=P)).then_inc(w["resid_in"], 16)

            @block.scalar
            def _(act):
                with nc.allow_non_contiguous_dma(reason="a column of the vector for each 128-row tile"):
                    act.dma_start(su[:], ins["SU_ug"].rearrange("(k p) -> p k", p=P)).then_inc(g["in_small"], 16)
                    act.dma_start(sud[:], ins["SU_dp"].rearrange("(k p) -> p k", p=P)).then_inc(g["in_small"], 16)
                    act.dma_start(w["gains"][:], ins["Wscale_ug"].rearrange("(k p) -> p k", p=P)).then_inc(g["in_small"], 16)
                act.dma_start(sdp[:], ins["Wscale_dp"].rearrange("(a n) -> a n", a=1).to_broadcast([P, D])).then_inc(g["in_small"], 16)
                act.wait_ge(g["zero"], 1)
                wo_rows = ins["w_o"].rearrange("(q j d) n -> j d q n", j=GH, d=DH)
                for j in range(GH):
                    act.dma_start(w["wo_raw"][32 * j:32 * j + DH, :, :], wo_rows[j]).then_inc(g["in_wo"], 16)

            @block.tensor
            def _(pe):
                pe.wait_ge(g["in_up"], 32)
                pe.wait_ge(g["neg"], 1)
                for n, (kind, a, b) in enumerate(jobs):
                    if n >= 8 and plain[n - 8]:
                        pe.wait_ge(g["dve_copy"], copied[n - 8])
                    elif n >= 8:
                        pe.wait_ge(g["full"], n - 7 - copied[n - 8])
                    if kind in need:
                        pe.wait_ge(g["dve_copy"], need[kind])
                    bank = ps[n % 8]
                    if kind == "tu":
                        for i in range(4):
                            last = nc.tensor.transpose(bank[:, P * i:P * i + P], up[:, a + i, P * b:P * b + P], c["ident"][:])
                    elif kind == "td":
                        pe.wait_ge(g["in_down"], 16)
                        for i in range(2):
                            for k in range(KD):
                                last = nc.tensor.transpose(bank[:, D * i + P * k:D * i + P * k + P],
                                                           down[:, k, P * (a + i):P * (a + i) + P], c["ident"][:])
                    elif kind == "to":
                        pe.wait_ge(g["in_attn"], 32)
                        for k in range(KD):
                            for m in range(KD):
                                last = nc.tensor.transpose(bank[:, D * k + P * m:D * k + P * m + P],
                                                           wout[:, m, P * k:P * k + P], c["ident"][:])
                    elif kind == "hu":
                        for k in range(KD):
                            h = negh if a and k else c["hadamard"]
                            last = nc.tensor.matmul(bank[:], h[:], upT[:, k, CH * b:CH * b + CH], start=(k == 0), stop=(k == KD - 1))
                    elif kind == "hd":
                        last = nc.tensor.matmul(bank[:], c["hadamard"][:], downT[:, a:a + 2, :].rearrange("p k n -> p (k n)"),
                                                start=True, stop=True)
                    else:
                        for m in range(KD):
                            for k in range(KD):
                                last = nc.tensor.matmul(bank[:, D * m:D * m + D], wv[:, k, P * m:P * m + P], woutT[:, k, :],
                                                        start=(k == 0), stop=(k == KD - 1))
                    last.then_inc(g["pe_done"], 1)

            @block.vector
            def _(dve):
                split = [0]

                def keep(make, high, low):
                    n = split[0]
                    split[0] += 1
                    if n >= 2:
                        dve.wait_ge(g["low"], n - 1)
                    last = make(full[:, n % 2, :])
                    last.then_inc(g["full"], 1)
                    dve.wait_ge(g["full"], n + 1)
                    last = nc.vector.tensor_copy(high, _like(full[:, n % 2, :], high)).then_inc(g["high"], 1)
                    dve.wait_ge(g["high"], n + 1)
                    nc.vector.tensor_tensor(low, _like(full[:, n % 2, :], high), high.bitcast(fp32), ALU.subtract).then_inc(g["low"], 1)

                nc.vector.memset(w["wo_raw"][:], 0.0).then_inc(g["zero"], 1)
                nc.vector.tensor_scalar(negh[:], c["hadamard"][:], -1.0, None, ALU.mult).then_inc(g["neg"], 1)
                dve.wait_ge(g["in_small"], 64)
                nc.vector.tensor_scalar(w["gain"][:], w["gains"][:], 1.0 / D ** 0.5, None, ALU.mult).then_inc(g["neg"], 1)
                nc.vector.tensor_scalar(sud32[:], sud[:], 1.0 / INTER ** 0.5, None, ALU.mult).then_inc(g["neg"], 1)
                dve.wait_ge(g["neg"], 3)
                for n, (kind, a, b) in enumerate(jobs):
                    dve.wait_ge(g["pe_done"], n + 1)
                    bank = ps[n % 8]
                    if kind == "tu":
                        nc.vector.tensor_copy(upT[:, b, P * a:P * a + CH], bank[:]).then_inc(g["dve_copy"], 1)
                    elif kind == "td":
                        nc.vector.tensor_copy(downT[:, a:a + 2, :], _like(bank[:], downT[:, a:a + 2, :])).then_inc(g["dve_copy"], 1)
                    elif kind == "to":
                        nc.vector.tensor_copy(woutT[:], _like(bank[:], woutT[:])).then_inc(g["dve_copy"], 1)
                    elif kind == "hu":
                        def make(dst):
                            return nc.vector.tensor_scalar(dst, bank[:], su[:, a:a + 1], None, ALU.mult)
                        keep(make, w["ug"][0][:, a, CH * b:CH * b + CH], w["ug"][1][:, a, CH * b:CH * b + CH])
                    elif kind == "hd":
                        nc.vector.tensor_copy(fly[0][:, a:a + 2, :], _like(bank[:], fly[0][:, a:a + 2, :])).then_inc(g["dve_copy"], 1)
                    else:
                        def make(dst):
                            return nc.vector.tensor_copy(dst, bank[:])
                        keep(make, w["ab"][0][:], w["ab"][1][:])
                count = copied[-1]
                src, width = 0, 1
                while width < KF:
                    dve.wait_ge(g["dve_copy"], count)
                    s = fly[src][:].rearrange("p (a two h) n -> p a two (h n)", two=2, h=width)
                    d = fly[1 - src][:].rearrange("p (a two h) n -> p a two (h n)", two=2, h=width)
                    nc.vector.tensor_tensor(d[:, :, 0, :], s[:, :, 0, :], s[:, :, 1, :], ALU.add).then_inc(g["dve_copy"], 1)
                    nc.vector.tensor_tensor(d[:, :, 1, :], s[:, :, 0, :], s[:, :, 1, :], ALU.subtract).then_inc(g["dve_copy"], 1)
                    src, width, count = 1 - src, 2 * width, count + 2
                dve.wait_ge(g["dve_copy"], count)
                for f in range(0, KF, 2):
                    def make(dst):
                        for i in range(2):
                            last = nc.vector.scalar_tensor_tensor(out=dst[:, D * i:D * i + D], in0=fly[src][:, f + i, :],
                                                                  scalar=sud32[:, f + i:f + i + 1], in1=sdp[:],
                                                                  op0=ALU.mult, op1=ALU.mult)
                        return last
                    keep(make, w["dn"][0][:, f:f + 2, :], w["dn"][1][:, f:f + 2, :])
                dve.wait_ge(g["in_wo"], 64)
                nc.vector.tensor_copy(w["wo"][0][:], w["wo_raw"][:]).then_inc(g["high"], 1)
                dve.wait_ge(g["high"], split[0] + 1)
                nc.vector.tensor_tensor(w["wo"][1][:], w["wo_raw"][:], w["wo"][0][:].bitcast(fp32), ALU.subtract).then_inc(g["low"], 1)
        clear(nc, list(g.values()))


def _like(flat, shaped):
    if len(shaped.shape) == 3:
        return flat.rearrange("p (a b) -> p a b", a=shaped.shape[1])
    return flat


PAIR = 2


def build_layers(nc, ctx, ins, out, c, w, o_all, loop):
    def sb(name, shape, dt=fp32):
        return ctx.enter_context(nc.sbuf_tensor(name, shape, dt))

    mid = [[sb(f"mid{i}{p}", [P, KF, CH], fp32r) for p in range(2)] for i in range(PAIR)]
    xT = [[sb(f"lxT{i}{p}", [P, KD, CH], fp32r) for p in range(2)] for i in range(PAIR)]
    xh = sb("xh", [P, TPC, D])
    silu = sb("silu", [P, 2, CH])
    prod = sb("prod", [P, 2, CH])
    stats = sb("lstats", [P, TPC, 6])
    mv = sb("lmv", [P, TPC, 2])
    rstd = sb("lrstd", [P, TPC, 2])
    psT = ctx.enter_context(nc.psum_tensor("psT2", [P, KD, CH], fp32))
    gate = [ctx.enter_context(nc.psum_tensor(f"gate{i}", [P, CH], fp32)) for i in range(2)]
    up = [ctx.enter_context(nc.psum_tensor(f"up{i}", [P, CH], fp32)) for i in range(2)]
    add = [ctx.enter_context(nc.psum_tensor(f"add{i}", [P, 2, D], fp32)) for i in range(2)]
    resid = w["resid"]
    names = ["o_high", "o_low", "add_done", "added", "stats_done", "aggregated", "eps_added", "rstd_done", "normed",
             "transposed", "high", "low", "gate_done", "up_done", "silu_done", "prod_done", "mid_high", "mid_low", "stored"]
    g = {n: ctx.enter_context(nc.semaphore("l_" + n)) for n in names}

    kinds = ["wo", "ffn", "attn", "ffn"]
    work = [("wo", i) for i in range(PAIR)]
    for kind in kinds[1:]:
        if kind == "ffn":
            work += [("ffn_up", i) for i in range(PAIR)] + [("ffn_down", i) for i in range(PAIR)]
        else:
            work += [("attn", i) for i in range(PAIR)]
    ADDS = TPC // 2
    adders = [n for n, (k, _) in enumerate(work) if k != "ffn_up"]
    users = [n for n, (k, _) in enumerate(work) if k in ("ffn_up", "attn")]
    ups = [n for n, (k, _) in enumerate(work) if k == "ffn_up"]
    norm_no = {n: i for i, n in enumerate(users)}
    add_no = {n: i for i, n in enumerate(adders)}
    up_no = {n: i for i, n in enumerate(ups)}

    def last_adder(n):
        return max(a for a in adders if a < n and work[a][1] == work[n][1])

    def last_user(n, kinds_):
        found = [m for m in range(n) if work[m][1] == work[n][1] and work[m][0] in kinds_]
        return found[-1] if found else None

    norms_after = {n: [] for n in range(len(work))}
    norms_within = {n: [] for n in range(len(work))}
    for u in users:
        n, k0 = last_adder(u), norm_no[u]
        if k0 == 0 or users[k0 - 1] <= n:
            norms_after[n].append(u)
        else:
            norms_within[users[k0 - 1]].append(u)

    def body(pair):
        def tile(i, t):
            return (pair * PAIR + i) * TPC + t

        def tiles(i, t, n):
            a = tile(i, t)
            return slice(a, a + n) if isinstance(pair, int) else bass.ds(a, n)

        def tokens(i):
            a = (pair * PAIR + i) * CH
            return slice(a, a + CH) if isinstance(pair, int) else bass.ds(a, CH)

        with nc.Block() as block:
            @block.tensor
            def _(pe):
                for n, (kind, i) in enumerate(work):
                    if kind in ("ffn_up", "attn"):
                        k0 = norm_no[n]
                        pe.wait_ge(g["normed"], TPC * (k0 + 1))
                        if k0:
                            pe.wait_ge(g["low"], k0)
                        for k in range(KD):
                            for t in range(TPC):
                                last = nc.tensor.transpose(psT[:, k, P * t:P * t + P], xh[:, t, P * k:P * k + P], c["ident"][:])
                        last.then_inc(g["transposed"], 1)
                        pe.wait_ge(g["low"], k0 + 1)
                    if kind == "ffn_up":
                        for f in range(KF):
                            u = KF * up_no[n] + f
                            if u >= 2:
                                pe.wait_ge(g["prod_done"], u - 1)
                            for which, banks, sem in ((1, gate, "gate_done"), (0, up, "up_done")):
                                steps = [(k, a, b) for k in range(KD) for a, b in PASSES]
                                for m, (k, a, b) in enumerate(steps):
                                    at = INTER * which + P * f
                                    last = nc.tensor.matmul(banks[u % 2][:], w["ug"][a][:, k, at:at + P], xT[i][b][:, k, :],
                                                            start=(m == 0), stop=(m == len(steps) - 1))
                                last.then_inc(g[sem], 1)
                        continue
                    left, right, kt = {"wo": (mid[i], w["wo"], NG), "ffn_down": (mid[i], w["dn"], KF),
                                       "attn": (xT[i], w["ab"], KD)}[kind]
                    if kind == "wo":
                        pe.wait_ge(g["o_low"], i + 1)
                    if kind == "ffn_down":
                        pe.wait_ge(g["mid_low"], KF * (up_no[last_user(n, ("ffn_up",))] + 1))
                    for h in range(ADDS):
                        r = ADDS * add_no[n] + h
                        if r >= 2:
                            pe.wait_ge(g["added"], r - 1)
                        for t in range(2):
                            at = P * (2 * h + t)
                            steps = [(k, a, b) for k in range(kt) for a, b in PASSES]
                            for m, (k, a, b) in enumerate(steps):
                                last = nc.tensor.matmul(add[r % 2][:, t, :], left[a][:, k, at:at + P], right[b][:, k, :],
                                                        start=(m == 0), stop=(m == len(steps) - 1))
                        last.then_inc(g["add_done"], 1)

            def high_part(act, n):
                k0 = norm_no[n]
                act.wait_ge(g["transposed"], k0 + 1)
                before = last_user(n, ("ffn_up", "attn"))
                if before is not None:
                    if work[before][0] == "ffn_up":
                        act.wait_ge(g["up_done"], KF * (up_no[before] + 1))
                    else:
                        act.wait_ge(g["add_done"], ADDS * (add_no[before] + 1))
                nc.scalar.copy(xT[work[n][1]][0][:], psT[:]).then_inc(g["high"], 1)

            def high_mid(act, i, u, f):
                act.wait_ge(g["prod_done"], u + 1)
                nc.scalar.copy(mid[i][0][:, f, :], prod[:, u % 2, :]).then_inc(g["mid_high"], 1)

            @block.scalar
            def _(act):
                for i in range(PAIR):
                    nc.scalar.copy(mid[i][0][:, 0:NG, :], o_all[:, :, tokens(i)]).then_inc(g["o_high"], 1)
                for n, (kind, i) in enumerate(work):
                    if n in norm_no:
                        high_part(act, n)
                    if kind == "ffn_up":
                        before = last_user(n, ("wo", "ffn_down"))
                        act.wait_ge(g["add_done"], ADDS * (add_no[before] + 1))
                        for f in range(KF):
                            u = KF * up_no[n] + f
                            act.wait_ge(g["gate_done"], u + 1)
                            if u >= 2:
                                act.wait_ge(g["prod_done"], u - 1)
                            nc.scalar.activation(silu[:, u % 2, :], gate[u % 2][:], ACT.Silu,
                                                 scale=w["gain"][:, KF + f:KF + f + 1]).then_inc(g["silu_done"], 1)
                            if f:
                                high_mid(act, i, u - 1, f - 1)
                        high_mid(act, i, u, f)

            @block.gpsimd
            def _(pool):
                def root(n):
                    k0 = norm_no[n]
                    pool.wait_ge(g["aggregated"], TPC * (k0 + 1))
                    nc.gpsimd.tensor_scalar(rstd[:, :, 0], mv[:, :, 1], EPS, None, ALU.add).then_inc(g["eps_added"], 1)
                    pool.wait_ge(g["eps_added"], k0 + 1)
                    nc.gpsimd.tensor_tensor(rstd[:, :, 1], rstd[:, :, 0], c["rootexp"][:], ALU.pow).then_inc(g["rstd_done"], 1)

                for n, (kind, i) in enumerate(work):
                    for m in norms_within[n] + norms_after[n]:
                        root(m)
                    if kind == "ffn_up":
                        for f in range(KF):
                            u = KF * up_no[n] + f
                            pool.wait_ge(g["mid_high"], u + 1)
                            nc.gpsimd.tensor_tensor(mid[i][1][:, f, :], prod[:, u % 2, :], mid[i][0][:, f, :].bitcast(fp32),
                                                    ALU.subtract).then_inc(g["mid_low"], 1)

            @block.vector
            def _(dve):
                for i in range(PAIR):
                    dve.wait_ge(g["o_high"], i + 1)
                    nc.vector.tensor_tensor(mid[i][1][:, 0:NG, :], o_all[:, :, tokens(i)], mid[i][0][:, 0:NG, :].bitcast(fp32),
                                            ALU.subtract).then_inc(g["o_low"], 1)

                def norm(n):
                    k0, i = norm_no[n], work[n][1]
                    if k0:
                        dve.wait_ge(g["normed"], TPC * k0)
                    for t in range(TPC):
                        nc.vector.bn_stats(stats[:, t, :], resid[:, tile(i, t), :]).then_inc(g["stats_done"], 1)
                    for t in range(TPC):
                        dve.wait_ge(g["stats_done"], TPC * k0 + t + 1)
                        nc.vector.bn_aggr(mv[:, t, :], stats[:, t, :]).then_inc(g["aggregated"], 1)
                    dve.wait_ge(g["rstd_done"], k0 + 1)
                    if k0:
                        dve.wait_ge(g["transposed"], k0)
                    for t in range(TPC):
                        nc.vector.tensor_scalar(xh[:, t, :], resid[:, tile(i, t), :], mv[:, t, 0:1],
                                                rstd[:, t, 1:2], ALU.subtract, ALU.mult).then_inc(g["normed"], 1)

                def low_part(n):
                    dve.wait_ge(g["high"], norm_no[n] + 1)
                    nc.vector.tensor_tensor(xT[work[n][1]][1][:], psT[:], xT[work[n][1]][0][:].bitcast(fp32),
                                            ALU.subtract).then_inc(g["low"], 1)

                for n, (kind, i) in enumerate(work):
                    if n in norm_no:
                        low_part(n)
                    for m in norms_within[n]:
                        norm(m)
                    if kind == "ffn_up":
                        for f in range(KF):
                            u = KF * up_no[n] + f
                            dve.wait_ge(g["silu_done"], u + 1)
                            dve.wait_ge(g["up_done"], u + 1)
                            if u >= 2:
                                dve.wait_ge(g["mid_low"], u - 1)
                            nc.vector.scalar_tensor_tensor(out=prod[:, u % 2, :], in0=up[u % 2][:], scalar=w["gain"][:, f:f + 1],
                                                           in1=silu[:, u % 2, :], op0=ALU.mult, op1=ALU.mult)\
                                .then_inc(g["prod_done"], 1)
                        continue
                    for h in range(ADDS):
                        r = ADDS * add_no[n] + h
                        dve.wait_ge(g["add_done"], r + 1)
                        at = tiles(i, 2 * h, 2)
                        nc.vector.tensor_tensor(resid[:, at, :], resid[:, at, :], add[r % 2][:], ALU.add).then_inc(g["added"], 1)
                    dve.wait_ge(g["added"], ADDS * (add_no[n] + 1))
                    for m in norms_after[n]:
                        norm(m)

            @block.sync
            def _(sp):
                for i in range(PAIR):
                    last = max(a for a in adders if work[a][1] == i)
                    sp.wait_ge(g["added"], ADDS * (add_no[last] + 1))
                    rows = out[0].rearrange("(t p) d -> p t d", p=P)
                    sp.dma_start(rows[:, tiles(i, 0, TPC), :], resid[:, tiles(i, 0, TPC), :]).then_inc(g["stored"], 16)
                sp.wait_ge(g["stored"], 16 * PAIR)
        clear(nc, list(g.values()))

    if loop:
        with nc.Fori(0, NCH // PAIR) as pair:
            body(pair)
    else:
        for pair in range(NCH // PAIR):
            body(pair)


def build(nc, x, w_q, w_k, w_v, w_o, weight_qkv, weight_out, SU_ug, SU_dp, Wscale_ug, Wscale_dp, W_up, W_gate, W_down, out,
          loop_attention=False, loop_layers=True):
    ins = dict(x=x, w_o=w_o, weight_qkv=weight_qkv, weight_out=weight_out, SU_ug=SU_ug, SU_dp=SU_dp,
               Wscale_ug=Wscale_ug, Wscale_dp=Wscale_dp, W_up=W_up, W_gate=W_gate, W_down=W_down)
    with ExitStack() as ctx:
        def sb(name, shape, dt=fp32, ctx=ctx):
            return ctx.enter_context(nc.sbuf_tensor(name, shape, dt))

        ident = sb("ident", [P, P])
        identb = sb("identb", [P, P], bf16)
        causal = sb("causal", [P, P], bf16)
        spread = sb("spread", [P, P])
        hadamard = sb("hadamard", [P, P])
        rootexp = sb("rootexp", [P, TPC])
        o_all = sb("o_all", [P, NG, S])
        with ExitStack() as attn:
            qs = sb("qs", [KM, HEADS, S], bf16, attn)
            ks = sb("ks", [KM, HEADS, S], bf16, attn)
            v_aug = sb("v_aug", [P, TILES, HEADS, VW], fp32, attn)
            ones = o_all[:, NG - 1, S - CH // 2:S].bitcast(bf16)
            tmp = o_all[:, 0, 0:P]
            build_constants(nc, ident, identb, causal, spread, hadamard, tmp, ones, rootexp)
            build_projections(nc, x, w_q, w_k, w_v, ident, rootexp, ones, qs, ks, v_aug, o_all)
            build_attention(nc, attn, dict(qs=qs, ks=ks, v_aug=v_aug, o_all=o_all, identb=identb, causal=causal,
                                           spread=spread), loop_attention)
        c = dict(ident=ident, hadamard=hadamard, rootexp=rootexp)
        w = dict(resid=sb("resid", [P, TILES, D]), gains=sb("gains", [P, 2 * KF]), gain=sb("gain", [P, 2 * KF]),
                 resid_in=ctx.enter_context(nc.semaphore("resid_in")), wo_raw=sb("wo_raw", [P, NG, D]))
        for name, shape in (("ug", [P, KD, 2 * INTER]), ("dn", [P, KF, D]), ("ab", [P, KD, D]), ("wo", [P, NG, D])):
            w[name] = [sb(f"{name}{i}", shape, fp32r) for i in range(2)]
        build_weights(nc, ins, c, w)
        with nc.Block() as block:
            @block.vector
            def _(dve):
                dve.wait_ge(w["resid_in"], 16)
        build_layers(nc, ctx, ins, out, c, w, o_all, loop_layers)


_INS = ['L0_attn_a_x', 'L0_attn_a_w_q', 'L0_attn_a_w_k', 'L0_attn_a_w_v', 'L0_attn_a_w_o', 'L0_attn_b_weight_qkv',
        'L0_attn_b_weight_out', 'L0_ffn_SU_ug', 'L0_ffn_SU_dp', 'L0_ffn_Wscale_ug', 'L0_ffn_Wscale_dp', 'L0_ffn_W_up',
        'L0_ffn_W_gate', 'L0_ffn_W_down']


def kernel(**inputs):
    import numpy as _np
    import concourse.bacc as _bacc
    from concourse import mybir as _mybir
    from concourse.bass_utils import run_bass_kernel_spmd as _run

    nc = _bacc.Bacc("TRN2", target_bir_lowering=False, num_devices=1)
    arrays, args = {}, []
    for name in _INS:
        a = _np.ascontiguousarray(inputs[name])
        arrays[f"in_{name}_dram"] = a
        args.append(nc.dram_tensor(f"in_{name}_dram", a.shape, _mybir.dt.from_np(a.dtype), kind="ExternalInput").ap())
    out = nc.dram_tensor("out_0_dram", (1, S, D), fp32, kind="ExternalOutput").ap()
    build(nc, *args, out)
    r = _run(nc, [arrays], core_ids=[0])
    return r.results[0]["out_0_dram"]
```

```python
import concourse.bass as bass
from concourse import mybir
from contextlib import ExitStack
import math

fp32 = mybir.dt.float32
fp32r = mybir.dt.float32r
bf16 = mybir.dt.bfloat16
ALU = mybir.AluOpType
ACT = mybir.ActivationFunctionType
AX = mybir.AxisListType

P = 128
S = 2048
D = 256
KD = D // P
HEADS = 16
DH = D // HEADS
INTER = 1024
KF = INTER // P
CH = 512
NCH = S // CH
TPC = CH // P
TILES = S // P
GH = 4
NG = HEADS // GH
FFN_SCALE = 64.0
EPS = 1e-5
MASKED = -3.0e38
PARTS = 3
Q_PARTS = (0, 1, 2, 0, 1, 0)
K_PARTS = (2, 1, 0, 1, 0, 0)
Q_RUNS = ((0, 0, 3), (3, 0, 2), (5, 0, 1))
K_RUNS = ((0, 0, 3), (3, 1, 2), (5, 2, 1))
KS = len(Q_PARTS) * DH
KM = KS + 2
VW = DH + 1
STACK_IN = 16 * 2 * len(Q_RUNS)
PASSES = ((0, 0), (0, 1), (1, 0))


def clear(nc, sems):
    nc.all_engine_barrier()
    for s in sems:
        nc.gpsimd.sem_clear(s)
    nc.all_engine_barrier()


def build_constants(nc, ident, identb, causal, ones, rootexp, first_loads):
    with ExitStack() as ctx:
        filled = ctx.enter_context(nc.semaphore("c_filled"))
        ready = ctx.enter_context(nc.semaphore("c_ready"))
        with nc.Block() as block:
            @block.gpsimd
            def _(pool):
                nc.gpsimd.memset(ident[:], 0.0).then_inc(filled, 1)
                nc.gpsimd.memset(identb[:], 0.0).then_inc(filled, 1)
                nc.gpsimd.memset(causal[:], 0.0).then_inc(filled, 1)
                nc.gpsimd.memset(ones[:], 1.0).then_inc(filled, 1)
                nc.gpsimd.memset(rootexp[:], -0.5).then_inc(filled, 1)
                pool.wait_ge(filled, 5)
                nc.gpsimd.affine_select(out=ident[:], in_=ident[:], compare_op=ALU.not_equal, fill=1.0, base=0,
                                        pattern=[[-1, P]], channel_multiplier=1).then_inc(ready, 1)
                nc.gpsimd.affine_select(out=identb[:], in_=identb[:], compare_op=ALU.not_equal, fill=1.0, base=0,
                                        pattern=[[-1, P]], channel_multiplier=1).then_inc(ready, 1)
                nc.gpsimd.affine_select(out=causal[:], in_=causal[:], compare_op=ALU.is_ge, fill=MASKED, base=0,
                                        pattern=[[-1, P]], channel_multiplier=1).then_inc(ready, 1)

            @block.sync
            def _(sp):
                first_loads()
        clear(nc, (filled, ready))


NU = 2 * KD
SLOTS = 5


def load_stack(sp, m, qs, ks, scratch, stored, stacked):
    c, u = divmod(m, NU)
    for i in range(KD):
        sp.wait_ge(stored[(m + i) % SLOTS], 16 * ((m + i) // SLOTS + 1))
    for block0, part0, n in Q_RUNS if u < KD else K_RUNS:
        rows = slice(DH * block0, DH * (block0 + n))
        sp.dma_start(qs[rows, c, :, :] if u < KD else ks[rows, :, CH * c:CH * c + CH],
                     scratch[u // KD, part0:part0 + n, :, CH * c:CH * c + CH]
                     .rearrange("a (d h) n -> (a d) h n", d=DH)).then_inc(stacked[c], 16)


def build_projections(nc, x, w_q, w_k, w_v, c0, qs, ks, v_aug, o_all, stacked, stored, scratch, load_vectors):
    ident, rootexp, ones, hadamard = c0["ident"], c0["rootexp"], c0["ones"], c0["hadamard"]
    UNITS = NU + TPC // 2
    lent = o_all[:].rearrange("p t d -> p (t d)")
    parts = lent[:, 0:SLOTS * 3 * CH // 2].bitcast(bf16).rearrange("p (u a n) -> p u a n", u=SLOTS, a=3)
    with ExitStack() as ctx:
        def sb(name, shape, dt=fp32):
            return ctx.enter_context(nc.sbuf_tensor(name, shape, dt))

        xin = sb("xin", [P, 2, TPC, D])
        wraw = sb("wraw", [P, 3, KD, D])
        rest = sb("rest", [P, 2, CH])
        xT = [sb(f"xT{i}", [P, KD, CH], fp32r) for i in range(2)]
        wsp = [sb(f"wsp{i}", [P, 3, KD, D], fp32r) for i in range(2)]
        stats = sb("stats1", [P, TPC, 6])
        mv = sb("mv1", [P, TPC, 2])
        rstd = sb("rstd1", [P, TPC, 2])
        psT = ctx.enter_context(nc.psum_tensor("psT1", [P, KD, CH], fp32))
        unit = [ctx.enter_context(nc.psum_tensor(f"unit{i}", [P, CH], fp32)) for i in range(UNITS)]

        names = ["x_in0", "x_in1", "w_in0", "w_in1", "w_in2", "w_high", "w_low", "stats_done", "aggregated", "eps_added", "rstd_done",
                 "normed", "transposed", "high_done", "low_done", "unit_done", "part1_done", "rest_done",
                 "part2_done", "parts_done", "v_done", "ones_in", "v_ones", "level"]
        sems = {n: ctx.enter_context(nc.semaphore("p_" + n)) for n in names}
        x_in = (sems["x_in0"], sems["x_in1"])
        g = sems
        tmp = sb("had_tmp", [P, P])

        def load_x(engine, c):
            engine.dma_start(xin[:, c % 2, :, :],
                             x[0, CH * c:CH * c + CH, :].rearrange("(t p) d -> p t d", p=P)).then_inc(x_in[c % 2], 16)

        def first_loads():
            load_x(nc.sync, 0)
            for n, w in enumerate((w_q, w_k, w_v)):
                nc.sync.dma_start(wraw[:, n, :, :], w.rearrange("(k p) n -> p k n", p=P)).then_inc(g[f"w_in{n}"], 16)
            load_x(nc.sync, 1)
            load_vectors()

        build_constants(nc, ident, c0["identb"], c0["causal"], ones, rootexp, first_loads)
        with nc.Block() as block:
            @block.sync
            def _(sp):
                for r in range(2):
                    sp.dma_start(ks[KS + r:KS + r + 1, :, :].rearrange("p h (b n) -> p (h b) n", n=CH),
                                 ones[64 * r:64 * r + 64, :]).then_inc(g["ones_in"], 16)
                for n in range(NU * NCH):
                    if n % KD == 1 and 3 <= n < NU * NCH - 1:
                        load_stack(sp, n - 3, qs, ks, scratch, stored, stacked)
                    c, u = divmod(n, NU)
                    sp.wait_ge(g["parts_done"], n + 1)
                    sp.dma_start(scratch[u // KD, :, P * (u % KD):P * (u % KD) + P, CH * c:CH * c + CH].rearrange("a p n -> p a n"),
                                 parts[:, n % SLOTS, :, :]).then_inc(stored[n % SLOTS], 16)
                sp.wait_ge(g["ones_in"], 32)

            def weight(n):
                views = [w[:, n, :, :] for w in (wraw, wsp[0], wsp[1])]
                if n == 2:
                    return views
                return [views[0].rearrange("p k (h d) -> p k d h", d=DH)] + [v.rearrange("p k (d h) -> p k d h", d=DH) for v in views[1:]]

            def lie(n, part):
                return part if n % NU < KD else PARTS - 1 - part

            def second_part(act, n):
                act.wait_ge(g["rest_done"], n + 1)
                nc.scalar.copy(parts[:, n % SLOTS, lie(n, 1), :], rest[:, n % 2, :]).then_inc(g["part2_done"], 1)

            def chunk(act, c):
                act.wait_ge(g["transposed"], c + 1)
                if c:
                    act.wait_ge(g["unit_done"], UNITS * c)
                nc.scalar.copy(xT[0][:], psT[:]).then_inc(g["high_done"], 1)
                for u in range(UNITS):
                    act.wait_ge(g["unit_done"], UNITS * c + u + 1)
                    if u and u <= NU:
                        second_part(act, NU * c + u - 1)
                    if u < NU:
                        n = NU * c + u
                        if n >= SLOTS:
                            act.wait_ge(stored[n % SLOTS], 16 * (n // SLOTS))
                        nc.scalar.copy(parts[:, n % SLOTS, lie(n, 0), :], unit[u][:]).then_inc(g["part1_done"], 1)
                    else:
                        if c == 0:
                            act.wait_ge(g["v_ones"], 1)
                        t = TPC * c + 2 * (u - NU)
                        nc.scalar.copy(v_aug[:, t:t + 2, :, 0:DH],
                                       unit[u][:].rearrange("p (t h d) -> p t h d", t=2, d=DH)).then_inc(g["v_done"], 1)

            @block.scalar
            def _(act):
                for n in range(3):
                    raw, high, _ = weight(n)
                    act.wait_ge(g[f"w_in{n}"], 16)
                    nc.scalar.copy(high, raw).then_inc(g["w_high"], 1)
                for c in range(NCH):
                    if c + 1 in range(2, NCH):
                        act.wait_ge(g["transposed"], c)
                        load_x(act, c + 1)
                    chunk(act, c)

            @block.gpsimd
            def _(pool):
                nc.gpsimd.memset(v_aug[:, :, :, DH:VW], 1.0).then_inc(g["v_ones"], 1)

                def root(c):
                    pool.wait_ge(g["aggregated"], TPC * (c + 1))
                    nc.gpsimd.tensor_scalar(rstd[:, :, 0], mv[:, :, 1], EPS, None, ALU.add).then_inc(g["eps_added"], 1)
                    pool.wait_ge(g["eps_added"], c + 1)
                    nc.gpsimd.tensor_tensor(rstd[:, :, 1], rstd[:, :, 0], rootexp[:], ALU.pow).then_inc(g["rstd_done"], 1)

                root(0)
                for c in range(NCH):
                    if c + 1 < NCH:
                        root(c + 1)
                    for u in range(NU):
                        n = NU * c + u
                        slot = n % SLOTS
                        pool.wait_ge(g["part2_done"], n + 1)
                        nc.gpsimd.tensor_tensor(parts[:, slot, lie(n, 2), :], rest[:, n % 2, :], parts[:, slot, lie(n, 1), :],
                                                ALU.subtract).then_inc(g["parts_done"], 1)

            @block.vector
            def _(dve):
                def statistics(c):
                    dve.wait_ge(x_in[c % 2], 16 * (c // 2 + 1))
                    if c:
                        dve.wait_ge(g["normed"], TPC * c)
                    for t in range(TPC):
                        nc.vector.bn_stats(stats[:, t, :], xin[:, c % 2, t, :]).then_inc(g["stats_done"], 1)
                    for t in range(TPC):
                        dve.wait_ge(g["stats_done"], TPC * c + t + 1)
                        nc.vector.bn_aggr(mv[:, t, :], stats[:, t, :]).then_inc(g["aggregated"], 1)

                def normalise(c):
                    dve.wait_ge(g["rstd_done"], c + 1)
                    for t in range(TPC):
                        nc.vector.tensor_scalar(xin[:, c % 2, t, :], xin[:, c % 2, t, :], mv[:, t, 0:1],
                                                rstd[:, t, 1:2], ALU.subtract, ALU.mult).then_inc(g["normed"], 1)

                def low_weight(n):
                    raw, high, low = weight(n)
                    dve.wait_ge(g["w_high"], n + 1)
                    nc.vector.tensor_tensor(low, raw, high.bitcast(fp32), ALU.subtract).then_inc(g["w_low"], 1)

                def hadamard_levels():
                    src, n, width = ident, 0, 1
                    while width < P:
                        dst = hadamard if src is not hadamard else tmp
                        a = src[:].rearrange("p (a two h) -> p a two h", two=2, h=width)
                        b = dst[:].rearrange("p (a two h) -> p a two h", two=2, h=width)
                        if n:
                            dve.wait_ge(g["level"], n)
                        nc.vector.tensor_tensor(b[:, :, 0, :], a[:, :, 0, :], a[:, :, 1, :], ALU.add).then_inc(g["level"], 1)
                        nc.vector.tensor_tensor(b[:, :, 1, :], a[:, :, 0, :], a[:, :, 1, :], ALU.subtract).then_inc(g["level"], 1)
                        src, n, width = dst, n + 2, 2 * width
                    assert src is hadamard

                statistics(0)
                low_weight(0)
                normalise(0)
                low_weight(1)
                low_weight(2)
                for c in range(NCH):
                    dve.wait_ge(g["high_done"], c + 1)
                    nc.vector.tensor_tensor(xT[1][:], psT[:], xT[0][:].bitcast(fp32), ALU.subtract).then_inc(g["low_done"], 1)
                    if c + 1 < NCH:
                        statistics(c + 1)
                    for u in range(NU):
                        n = NU * c + u
                        dve.wait_ge(g["part1_done"], n + 1)
                        if n >= 2:
                            dve.wait_ge(g["parts_done"], n - 1)
                        nc.vector.tensor_tensor(rest[:, n % 2, :], unit[u][:], parts[:, n % SLOTS, lie(n, 0), :],
                                                ALU.subtract).then_inc(g["rest_done"], 1)
                    if c + 1 < NCH:
                        normalise(c + 1)
                    if c == 1:
                        hadamard_levels()

            @block.tensor
            def _(pe):
                def transposes(c):
                    pe.wait_ge(g["normed"], TPC * (c + 1))
                    if c:
                        pe.wait_ge(g["low_done"], c)
                    for k in range(KD):
                        for t in range(TPC):
                            last = nc.tensor.transpose(psT[:, k, P * t:P * t + P], xin[:, c % 2, t, P * k:P * k + P], ident[:])
                    last.then_inc(g["transposed"], 1)

                transposes(0)
                for c in range(NCH):
                    pe.wait_ge(g["low_done"], c + 1)
                    for u in range(UNITS):
                        if c == 0 and (u == NU or u < NU and u % KD == 0):
                            pe.wait_ge(g["w_low"], u // KD + 1)
                        if c and u < NU:
                            pe.wait_ge(g["rest_done"], NU * (c - 1) + u + 1)
                        if c and u >= NU:
                            pe.wait_ge(g["v_done"], (UNITS - NU) * (c - 1) + u - NU + 1)
                        steps = [(k, a, b) for k in range(KD) for a, b in PASSES]
                        if u < NU:
                            m = u % KD
                            for i, (k, a, b) in enumerate(steps):
                                last = nc.tensor.matmul(unit[u][:], wsp[a][:, u // KD, k, P * m:P * m + P], xT[b][:, k, :],
                                                        start=(i == 0), stop=(i == len(steps) - 1))
                        else:
                            for t in range(2):
                                at = P * (2 * (u - NU) + t)
                                for i, (k, a, b) in enumerate(steps):
                                    last = nc.tensor.matmul(unit[u][:, D * t:D * t + D], xT[a][:, k, at:at + P], wsp[b][:, 2, k, :],
                                                            start=(i == 0), stop=(i == len(steps) - 1))
                        last.then_inc(g["unit_done"], 1)
                    if c + 1 < NCH:
                        transposes(c + 1)
        clear(nc, list(sems.values()))


ITEMS = [(group, c) for group in range(NG) for c in (range(NCH) if group < NG - 1 else reversed(range(NCH)))]
PIECES = [(i, qb, j, k0, min(CH, P * (qb + 1) - k0)) for i, (_, c) in enumerate(ITEMS)
          for qb in range(TPC * c, TPC * c + TPC) for j in range(GH) for k0 in range(0, P * (qb + 1), CH)]
QUADS = [(i, kb, P * max(0, kb - TPC * c), CH - P * max(0, kb - TPC * c))
         for i, (_, c) in enumerate(ITEMS) for kb in range(TPC * (c + 1))]
LAST_QUAD = {q[0]: n for n, q in enumerate(QUADS)}
LAST_PIECE = {p[0]: n for n, p in enumerate(PIECES)}
FIRST_PIECE = {p[0]: n for n, p in reversed(list(enumerate(PIECES)))}
ST_BANKS = 3
MAX_BANKS = 4
P_SLOTS = 12
ROWS_IN = 16 * 2
TURNS = [("down", f, 0) for f in range(0, KF, 2)] + [("up", f, k) for k in range(KD) for f in range(0, 2 * KF, 4)]
TURNS += [("out", 0, 0)]
LEAD = 64 * CH


def plan():
    hop, act_wait, act_col, dve_wait, dve_col, rows_in = 200.0, 50.0, 1 / 1.2, 65.0, 1 / 0.96, 3000.0
    work = []
    for n, p in enumerate(PIECES):
        if p[0] and n == FIRST_PIECE[p[0]] + 3:
            work.append(("T", p[0] - 1))
        work.append(("M", n))
    work.append(("T", len(ITEMS) - 1))
    work.reverse()
    pe = act = dve = pool = 0.0
    exp_at, rows_at, maxima_at, read_at, scaled_at = {}, {}, {}, {}, {}
    st_free, max_free, turns, order = [], [], [], []
    s = v = w = done = seen = 0
    while s < GH * len(QUADS) or work or v < len(QUADS) or turns or w < len(TURNS):
        can = {}
        if s < GH * len(QUADS) and (s < P_SLOTS or GH * v > s - P_SLOTS):
            i, kb, _, nq = QUADS[s // GH]
            if i in rows_at:
                can["S"] = max(pe, rows_at[i] if kb == 0 else 0, st_free[-ST_BANKS] if len(st_free) >= ST_BANKS else 0)
        if work:
            kind, n = work[-1]
            waiting = s < GH * len(QUADS) and QUADS[s // GH][0] not in rows_at
            if kind == "T" or done < seen + LEAD or waiting or s == GH * len(QUADS):
                can[kind] = max(pe, max_free[-MAX_BANKS] if len(max_free) >= MAX_BANKS else 0,
                                maxima_at[n] if kind == "T" else 0)
        if v < len(QUADS) and s >= GH * (v + 1):
            i, kb, _, nq = QUADS[v]
            if kb or not i or i - 1 in read_at:
                can["V"] = max(pe, exp_at[v], read_at[i - 1] if kb == 0 and i else 0)
        if turns:
            can["R"] = max(pe, st_free[-ST_BANKS], read_at[turns[0]])
        if not work and w < len(TURNS) and v >= LAST_QUAD[len(ITEMS) - GH + 1]:
            can["W"] = max(pe, max_free[-MAX_BANKS])
        now = min(can.values())
        ready = [k for k in ("T", "R", "S", "M", "V", "W") if k in can and can[k] <= now + 1]
        act_left, dve_left = act - pe, dve - pe
        if ready[0] in "TR":
            kind = ready[0]
        elif "S" in ready and act_left < 100 and not ("M" in ready and dve_left < act_left):
            kind = "S"
        elif "M" in ready and dve_left < 100:
            kind = "M"
        elif "V" in ready and (ready[0] == "V" or (act_left > 900 and (dve_left > 900 or not work))):
            kind = "V"
        elif "S" in ready and "M" in ready:
            kind = "S" if act_left <= dve_left else "M"
        else:
            kind = ready[0]
        pe = now
        if kind == "S":
            i, kb, _, nq = QUADS[s // GH]
            pe += nq / 2.4
            act = max(act, pe + hop) + act_wait + act_col * nq
            st_free.append(act + hop)
            exp_at[s // GH] = act + hop
            if kb >= TPC * ITEMS[i][1]:
                pool = max(pool, act + hop) + 244
                exp_at[s // GH] = pool + hop
            order.append(("S", s // GH, s % GH))
            s, seen = s + 1, seen + nq
        elif kind == "M":
            n = work.pop()[1]
            i, _, _, _, nk = PIECES[n]
            pe += nk / 2.4
            dve = max(dve, pe + hop) + dve_wait + dve_col * nk
            max_free.append(dve + hop)
            done += nk
            if LAST_PIECE[i] == n:
                dve += 800
                maxima_at[i] = dve + hop
            order.append(("M", n))
        elif kind == "T":
            i = work.pop()[1]
            pe += 60
            dve = max(dve, pe + hop) + 2 * dve_wait
            max_free.append(dve + hop)
            rows_at[i] = dve + rows_in
            order.append(("T", i))
        elif kind == "W":
            pe += 4 * 4 * P / 2.4
            dve = max(dve, pe + hop) + dve_wait + dve_col * CH
            max_free.append(dve + hop)
            order.append(("W", w))
            w += 1
        elif kind == "V":
            i, _, _, nq = QUADS[v]
            pe += 2 * nq / 1.2 + 60
            if LAST_QUAD[i] == v:
                act = max(act, pe + hop, scaled_at.get(i - 1, 0)) + act_wait + act_col * CH
                read_at[i] = act + hop
                turns.append(i)
            order.append(("V", v))
            v += 1
        else:
            i = turns.pop(0)
            pe += 440
            dve = max(dve, pe + hop) + 700
            scaled_at[i] = dve + hop
            st_free.append(dve + hop)
            order.append(("R", i))
    return order


def later_loads(ins, w):
    up, down, resid = w["up_raw"], w["down_raw"], w["resid"]
    half = KF // 2
    loads = []
    for name, at in (("W_up", 0), ("W_gate", KF)):
        rows = ins[name].rearrange("(f p) j -> p f j", p=P)
        loads += [(up[:, at + f:at + f + half, :], rows[:, f:f + half, :], "up") for f in (0, half)]
    rows = ins["W_down"].rearrange("(k p) j -> p k j", p=P)
    loads += [(down[:, k, :], rows[:, k, :], "down") for k in range(KD)]
    loads += [(w["wv_raw"][:], ins["weight_qkv"][2 * D:3 * D, :].rearrange("(k p) j -> p k j", p=P), "attn"),
              (w["wout_raw"][:], ins["weight_out"].rearrange("(k p) j -> p k j", p=P), "attn"),
              (w["wo_raw"][:], ins["w_o"].rearrange("(k p) n -> p k n", p=P), "wo")]
    rows = ins["x"][0].rearrange("(t p) d -> p t d", p=P)
    return loads + [(resid[:, t:t + TPC, :], rows[:, t:t + TPC, :], "resid") for t in range(0, TILES, TPC)]


def load_vectors(nc, ins, w, loaded):
    with nc.allow_non_contiguous_dma(reason="single numbers, few"):
        for name, src in (("su", "SU_ug"), ("sud", "SU_dp"), ("gains", "Wscale_ug")):
            nc.sync.dma_start(w[name][:], ins[src].rearrange("(k p) -> p k", p=P)).then_inc(loaded["small"], 16)
    nc.sync.dma_start(w["sdp"][:], ins["Wscale_dp"].rearrange("(a n) -> a n", a=1).to_broadcast([P, D])).then_inc(loaded["small"], 16)


def build_attention(nc, ctx, t, stacked, stored, scratch, loads, loaded, w):
    def sb(name, shape, dt=fp32):
        return ctx.enter_context(nc.sbuf_tensor(name, shape, dt))

    qs, ks, v_aug, o_all = t["qs"], t["ks"], t["v_aug"], t["o_all"]
    ident, identb, causal = t["ident"], t["identb"], t["causal"]
    mx = sb("mx", [P, GH, TPC, NCH])
    mtmp = sb("mtmp", [P, GH, TPC])
    mparts = sb("mparts", [P, 2 * GH * TPC], bf16)
    mrow = sb("mrow", [32, P], bf16)
    probs = sb("probs", [P, P_SLOTS, CH])
    oraw = sb("oraw", [P, CH])
    rec = sb("rec", [P, TPC, GH])
    smax = [ctx.enter_context(nc.psum_tensor(f"smax{i}", [P, CH], fp32)) for i in range(MAX_BANKS)]
    st = [ctx.enter_context(nc.psum_tensor(f"st{i}", [P, CH], fp32)) for i in range(ST_BANKS)]
    ops = ctx.enter_context(nc.psum_tensor("ops", [P, CH], fp32))
    names = ["smax_done", "smax_read", "mparts_done", "max_row", "score_done", "exp_done", "masked", "pv_done", "o_read",
             "turned", "inverted", "scaled", "combined", "zeroed"]
    g = {n: ctx.enter_context(nc.semaphore("a_" + n)) for n in names}

    assert nc.sbuf_base <= w["up_at"]
    order = plan()
    smax_at = {o: n for n, o in enumerate(o for o in order if o[0] in "MTW")}
    st_at = {o: n for n, o in enumerate(o for o in order if o[0] in "SR")}
    frees, exps, divides = [], 0, 0
    for o in st_at:
        if o[0] == "S":
            exps += 1
            frees.append(("exp_done", exps))
        else:
            divides += 1
            frees.append(("scaled", divides))
    diag = [kb >= TPC * ITEMS[i][1] for i, kb, _, _ in QUADS]
    masks_before = [GH * sum(diag[:n]) for n in range(len(QUADS) + 1)]

    with nc.Block() as block:
        @block.tensor
        def _(pe):
            pe.wait_ge(g["zeroed"], 1)
            nc.tensor.matmul(ops[:], probs[:, 0, 0:P], probs[:, 0, :], start=True, stop=True)
            for o in order:
                if o[0] in "MTW":
                    n = smax_at[o]
                    bank = smax[n % MAX_BANKS]
                    if n >= MAX_BANKS:
                        pe.wait_ge(g["smax_read"], n - MAX_BANKS + 1)
                    if o[0] == "M":
                        i, qb, j, k0, nk = PIECES[o[1]]
                        group, c = ITEMS[i]
                        if group == 0 and o[1] == FIRST_PIECE[i]:
                            pe.wait_ge(stacked[c], STACK_IN)
                        masked = k0 + nk == P * (qb + 1)
                        last = nc.tensor.matmul(bank[:, 0:nk], qs[0:KS, c, GH * group + j, P * (qb % TPC):P * (qb % TPC) + P],
                                                ks[0:KS, GH * group + j, k0:k0 + nk], start=True, stop=not masked)
                        if masked:
                            last = nc.tensor.matmul(bank[:, nk - P:nk], identb[:], causal[:], start=False, stop=True)
                    elif o[0] == "W":
                        kind, f, k = TURNS[o[1]]
                        if kind == "up":
                            pe.wait_ge(loaded["up"], 64)
                            blocks = [w["up_raw"][:, f + i, P * k:P * k + P] for i in range(4)]
                        elif kind == "down":
                            pe.wait_ge(loaded["down"], 32)
                            blocks = [w["down_raw"][:, j, P * (f + i):P * (f + i) + P] for i in range(2) for j in range(KD)]
                        else:
                            pe.wait_ge(loaded["attn"], 32)
                            blocks = [w["wout_raw"][:, j, P * i:P * i + P] for i in range(KD) for j in range(KD)]
                        for i, block_in in enumerate(blocks):
                            last = nc.tensor.transpose(bank[:, P * i:P * i + P], block_in, ident[:])
                    else:
                        pe.wait_ge(g["mparts_done"], o[1] + 1)
                        last = nc.tensor.transpose(bank[0:32, 0:P // 2].bitcast(bf16), mparts[:], identb[:])
                    last.then_inc(g["smax_done"], 1)
                elif o[0] == "S":
                    _, n, j = o
                    i, kb, q0, nq = QUADS[n]
                    group, c = ITEMS[i]
                    use = st_at[o]
                    if use >= ST_BANKS:
                        pe.wait_ge(g[frees[use - ST_BANKS][0]], frees[use - ST_BANKS][1])
                    if j == 0 and kb == 0:
                        pe.wait_ge(g["max_row"], ROWS_IN * (i + 1))
                    head = GH * group + j
                    nc.tensor.matmul(st[use % ST_BANKS][:, 0:nq], ks[0:KM, head, P * kb:P * kb + P],
                                     qs[0:KM, c, head, q0:CH], start=True, stop=True).then_inc(g["score_done"], 1)
                elif o[0] == "V":
                    n = o[1]
                    i, kb, q0, nq = QUADS[n]
                    group, c = ITEMS[i]
                    if kb == 0 and i:
                        pe.wait_ge(g["o_read"], i)
                    pe.wait_ge(g["exp_done"], GH * (n + 1))
                    if diag[n]:
                        pe.wait_ge(g["masked"], masks_before[n + 1])
                    for j in range(GH):
                        u = GH * n + j
                        nc.tensor.matmul(ops[32 * j:32 * j + VW, q0:CH], v_aug[:, kb, GH * group + j, :],
                                         probs[:, u % P_SLOTS, 0:nq],
                                         start=(kb == 0), stop=(kb == TPC * (c + 1) - 1)).then_inc(g["pv_done"], 1)
                else:
                    use = st_at[o]
                    pe.wait_ge(g[frees[use - ST_BANKS][0]], frees[use - ST_BANKS][1])
                    pe.wait_ge(g["o_read"], o[1] + 1)
                    for b in range(TPC):
                        last = nc.tensor.transpose(st[use % ST_BANKS][:, P * b:P * b + P], oraw[:, P * b:P * b + P], ident[:])
                    last.then_inc(g["turned"], 1)

        @block.scalar
        def _(act):
            later = list(loads)
            for o in order:
                if o[0] == "S":
                    _, n, j = o
                    i, kb, q0, nq = QUADS[n]
                    group = ITEMS[i][0]
                    u = GH * n + j
                    act.wait_ge(g["score_done"], u + 1)
                    if group == NG - 1 and j == 0 and later and (later[0][2] not in ("wo", "resid") or ITEMS[i][1] < NCH - 1):
                        dst, src, name = later.pop(0)
                        act.dma_start(dst, src).then_inc(loaded[name], 16)
                    if u >= P_SLOTS:
                        act.wait_ge(g["pv_done"], u - P_SLOTS + 1)
                    nc.scalar.activation(probs[:, u % P_SLOTS, 0:nq], st[st_at[o] % ST_BANKS][:, 0:nq], ACT.Exp,
                                         scale=DH ** -0.5).then_inc(g["exp_done"], 1)
                elif o[0] == "V" and LAST_QUAD[QUADS[o[1]][0]] == o[1]:
                    i = QUADS[o[1]][0]
                    act.wait_ge(g["pv_done"], GH * (o[1] + 1))
                    if i:
                        act.wait_ge(g["scaled"], i)
                    nc.scalar.copy(oraw[:], ops[:]).then_inc(g["o_read"], 1)

        @block.vector
        def _(dve):
            nc.vector.memset(probs[:, 0, :], 0.0).then_inc(g["zeroed"], 1)
            reads = 0
            combined = 0
            for o in order:
                if o[0] == "M":
                    i, qb, j, k0, nk = PIECES[o[1]]
                    c = ITEMS[i][1]
                    n = smax_at[o]
                    if i and o[1] == FIRST_PIECE[i]:
                        dve.wait_ge(g["mparts_done"], i)
                    dve.wait_ge(g["smax_done"], n + 1)
                    nc.vector.reduce_max(mx[:, j, qb % TPC, k0 // CH:k0 // CH + 1], smax[n % MAX_BANKS][:, 0:nk], AX.X)\
                        .then_inc(g["smax_read"], 1)
                    reads += 1
                    if o[1] == LAST_PIECE[i]:
                        dve.wait_ge(g["smax_read"], reads)
                        high = mparts[:, 0:GH * TPC].rearrange("p (j q) -> p j q", j=GH)
                        low = mparts[:, GH * TPC:2 * GH * TPC].rearrange("p (j q) -> p j q", j=GH)
                        m = mx[:, :, :, 0]
                        if c:
                            nc.vector.reduce_max(mtmp[:], mx[:, :, :, 0:c + 1], AX.X).then_inc(g["combined"], 1)
                            combined += 1
                            dve.wait_ge(g["combined"], combined)
                            m = mtmp[:]
                        nc.vector.tensor_scalar(high, m, -1.0, None, ALU.mult).then_inc(g["combined"], 1)
                        combined += 1
                        dve.wait_ge(g["combined"], combined)
                        nc.vector.scalar_tensor_tensor(out=low, in0=m, scalar=-1.0, in1=high, op0=ALU.mult,
                                                       op1=ALU.subtract).then_inc(g["mparts_done"], 1)
                elif o[0] == "W":
                    kind, f, k = TURNS[o[1]]
                    n = smax_at[o]
                    if kind == "up":
                        dst = w["upT"][:, k, P * f:P * f + CH]
                    else:
                        dst = w["downT"][:, f:f + 2, :] if kind == "down" else w["woutT"][:]
                    dve.wait_ge(g["smax_done"], n + 1)
                    nc.vector.tensor_copy(dst, _like(smax[n % MAX_BANKS][:], dst)).then_inc(g["smax_read"], 1)
                    reads += 1
                elif o[0] == "T":
                    n = smax_at[o]
                    dve.wait_ge(g["smax_done"], n + 1)
                    if o[1]:
                        dve.wait_ge(g["max_row"], ROWS_IN * o[1])
                    nc.vector.tensor_copy(mrow[:], smax[n % MAX_BANKS][0:32, 0:P // 2].bitcast(bf16)).then_inc(g["smax_read"], 1)
                    reads += 1
                elif o[0] == "R":
                    i = o[1]
                    group, c = ITEMS[i]
                    sums = st[st_at[o] % ST_BANKS][:].rearrange("p (t j d) -> p t j d", t=TPC, j=GH)
                    dve.wait_ge(g["turned"], i + 1)
                    if i:
                        dve.wait_ge(g["scaled"], i)
                    else:
                        for slot in range(SLOTS):
                            dve.wait_ge(stored[slot], 16 * len(range(slot, NU * NCH, SLOTS)))
                    nc.vector.reciprocal(rec[:], sums[:, :, :, DH]).then_inc(g["inverted"], 1)
                    dve.wait_ge(g["inverted"], i + 1)
                    dst = o_all[:, TPC * c:TPC * c + TPC, GH * DH * group:GH * DH * group + GH * DH]
                    nc.vector.tensor_tensor(dst.rearrange("p t (j d) -> p t j d", j=GH), sums[:, :, :, 0:DH],
                                            rec[:].unsqueeze(3).to_broadcast([P, TPC, GH, DH]), ALU.mult).then_inc(g["scaled"], 1)

        @block.gpsimd
        def _(pool):
            for n, (i, kb, q0, nq) in enumerate(QUADS):
                if diag[n]:
                    for j in range(GH):
                        u = GH * n + j
                        pool.wait_ge(g["exp_done"], u + 1)
                        blk = probs[:, u % P_SLOTS, 0:P]
                        nc.gpsimd.affine_select(out=blk, in_=blk, compare_op=ALU.is_ge, fill=0.0, base=0,
                                                pattern=[[1, P]], channel_multiplier=-1).then_inc(g["masked"], 1)

        @block.sync
        def _(sp):
            for m in (NU * NCH - 2 * KD, NU * NCH - KD):
                load_stack(sp, m, qs, ks, scratch, stored, stacked)
            for i, (group, c) in enumerate(ITEMS):
                sp.wait_ge(g["smax_read"], smax_at[("T", i)] + 1)
                for r in range(2):
                    dst = qs[KS + r:KS + r + 1, c, GH * group:GH * group + GH, :].rearrange("p j (b q) -> p (j b) q", q=P)
                    sp.dma_start(dst, mrow[GH * TPC * r:GH * TPC * (r + 1), :]).then_inc(g["max_row"], 16)
            sp.wait_ge(g["max_row"], ROWS_IN * len(ITEMS))
    clear(nc, list(g.values()))


def build_weights(nc, c, w, loaded):
    with ExitStack() as ctx:
        def sb(name, shape, dt=fp32):
            return ctx.enter_context(nc.sbuf_tensor(name, shape, dt))

        assert nc.sbuf_base == w["raw_at"]
        sb("raw_room", [P, w["raw_room"] // 4])
        wv, upT, downT, woutT, su, sud, sdp = (w[n] for n in ("wv_raw", "upT", "downT", "woutT", "su", "sud", "sdp"))
        fly = [sb(f"fly{i}", [P, KF, D]) for i in range(2)]
        negh = sb("negh", [P, P])
        sud32 = sb("sud32", [P, KF])
        ps = [ctx.enter_context(nc.psum_tensor(f"wps{i}", [P, CH], fp32)) for i in range(8)]
        names = ["neg", "scales", "pe_done", "copied", "high", "low", "level", "dn_high", "dn_low", "wo_high", "wo_low"]
        g = {n: ctx.enter_context(nc.semaphore("w_" + n)) for n in names}
        HD = KF // 2
        jobs = [("hd", f, 0) for f in range(0, KF, 2)] + [("ab", 0, 0)]
        jobs += [("hu", a, f) for a in range(KD) for f in range(2 * INTER // CH)]

        def target(n):
            kind, a, b = jobs[n]
            return [w["ug"][i][:, a, CH * b:CH * b + CH] if kind == "hu" else w["ab"][i][:] for i in range(2)]

        with nc.Block() as block:
            @block.tensor
            def _(pe):
                for n, (kind, a, b) in enumerate(jobs):
                    if n >= 8 + HD:
                        pe.wait_ge(g["low"], n - 8 - HD + 1)
                    elif n >= 8:
                        pe.wait_ge(g["copied"], n - 8 + 1)
                    bank = ps[n % 8]
                    if kind == "hd":
                        last = nc.tensor.matmul(bank[:], c["hadamard"][:], downT[:, a:a + 2, :].rearrange("p k n -> p (k n)"),
                                                start=True, stop=True)
                    elif kind == "ab":
                        for m in range(KD):
                            for k in range(KD):
                                last = nc.tensor.matmul(bank[:, D * m:D * m + D], wv[:, k, P * m:P * m + P], woutT[:, k, :],
                                                        start=(k == 0), stop=(k == KD - 1))
                    else:
                        pe.wait_ge(g["neg"], 1)
                        for k in range(KD):
                            h = negh if a and k else c["hadamard"]
                            last = nc.tensor.matmul(bank[:], h[:], upT[:, k, CH * b:CH * b + CH], start=(k == 0), stop=(k == KD - 1))
                    last.then_inc(g["pe_done"], 1)

            @block.scalar
            def _(act):
                act.wait_ge(loaded["wo"], 16)
                nc.scalar.copy(w["wo"][0][:], w["wo_raw"][:]).then_inc(g["wo_high"], 1)
                act.wait_ge(loaded["small"], 64)
                for n, (kind, a, b) in enumerate(jobs):
                    if kind != "hd":
                        high = target(n)[0]
                        act.wait_ge(g["pe_done"], n + 1)
                        nc.scalar.activation(high, _like(ps[n % 8][:], high), ACT.Identity,
                                             scale=su[:, a:a + 1] if kind == "hu" else 1.0).then_inc(g["high"], 1)
                    if n == len(jobs) - 4:
                        act.wait_ge(g["level"], 6)
                        act.wait_ge(g["scales"], 2)
                        for f in range(KF):
                            nc.scalar.activation(w["dn"][0][:, f, :], fly[1][:, f, :], ACT.Identity,
                                                 scale=sud32[:, f:f + 1]).then_inc(g["dn_high"], 1)

            @block.vector
            def _(dve):
                nc.vector.tensor_scalar(negh[:], c["hadamard"][:], -1.0, None, ALU.mult).then_inc(g["neg"], 1)
                dve.wait_ge(loaded["small"], 64)
                nc.vector.tensor_scalar(w["gain"][:], w["gains"][:], 1.0 / D ** 0.5, None, ALU.mult).then_inc(g["scales"], 1)
                nc.vector.tensor_scalar(sud32[:], sud[:], 1.0 / INTER ** 0.5, None, ALU.mult).then_inc(g["scales"], 1)
                for n in range(HD):
                    dve.wait_ge(g["pe_done"], n + 1)
                    nc.vector.tensor_tensor(fly[0][:, 2 * n:2 * n + 2, :], ps[n][:].rearrange("p (f n) -> p f n", f=2),
                                            sdp[:].unsqueeze(1).to_broadcast([P, 2, D]), ALU.mult).then_inc(g["copied"], 1)
                dve.wait_ge(g["copied"], HD)
                src, width, count = 0, 1, 0
                while width < KF:
                    if count:
                        dve.wait_ge(g["level"], count)
                    s = fly[src][:].rearrange("p (a two h) n -> p a two (h n)", two=2, h=width)
                    d = fly[1 - src][:].rearrange("p (a two h) n -> p a two (h n)", two=2, h=width)
                    nc.vector.tensor_tensor(d[:, :, 0, :], s[:, :, 0, :], s[:, :, 1, :], ALU.add).then_inc(g["level"], 1)
                    nc.vector.tensor_tensor(d[:, :, 1, :], s[:, :, 0, :], s[:, :, 1, :], ALU.subtract).then_inc(g["level"], 1)
                    src, width, count = 1 - src, 2 * width, count + 2
                for n in range(HD, len(jobs)):
                    kind, a, b = jobs[n]
                    high, low = target(n)
                    dve.wait_ge(g["high"], n - HD + 1)
                    if kind == "hu":
                        nc.vector.scalar_tensor_tensor(out=low, in0=ps[n % 8][:], scalar=su[:, a:a + 1], in1=high.bitcast(fp32),
                                                       op0=ALU.mult, op1=ALU.subtract).then_inc(g["low"], 1)
                    else:
                        nc.vector.tensor_tensor(low, _like(ps[n % 8][:], low), high.bitcast(fp32), ALU.subtract).then_inc(g["low"], 1)
                for f in range(KF):
                    dve.wait_ge(g["dn_high"], f + 1)
                    nc.vector.scalar_tensor_tensor(out=w["dn"][1][:, f, :], in0=fly[1][:, f, :], scalar=sud32[:, f:f + 1],
                                                   in1=w["dn"][0][:, f, :].bitcast(fp32), op0=ALU.mult, op1=ALU.subtract)\
                        .then_inc(g["dn_low"], 1)

            @block.gpsimd
            def _(pool):
                pool.wait_ge(g["wo_high"], 1)
                nc.gpsimd.tensor_tensor(w["wo"][1][:], w["wo_raw"][:], w["wo"][0][:].bitcast(fp32), ALU.subtract).then_inc(g["wo_low"], 1)
        clear(nc, list(g.values()))


def _like(flat, shaped):
    if len(shaped.shape) == 3:
        return flat.rearrange("p (a b) -> p a b", a=shaped.shape[1])
    return flat


PAIR = 2


def build_layers(nc, ctx, ins, out, c, w, o_all, loop):
    def sb(name, shape, dt=fp32):
        return ctx.enter_context(nc.sbuf_tensor(name, shape, dt))

    mid = [[sb(f"mid{i}{p}", [P, KF, CH], fp32r) for p in range(2)] for i in range(PAIR)]
    xT = [[sb(f"lxT{i}{p}", [P, KD, CH], fp32r) for p in range(2)] for i in range(PAIR)]
    heads = sb("heads", [P, PAIR, TPC, D])
    xh = sb("xh", [P, TPC, D])
    silu = sb("silu", [P, 2, CH])
    prod = sb("prod", [P, 2, CH])
    stats = sb("lstats", [P, TPC, 6])
    mv = sb("lmv", [P, TPC, 2])
    rstd = sb("lrstd", [P, TPC, 2])
    psT = ctx.enter_context(nc.psum_tensor("psT2", [P, KD, CH], fp32))
    gate = [ctx.enter_context(nc.psum_tensor(f"gate{i}", [P, CH], fp32)) for i in range(2)]
    up = [ctx.enter_context(nc.psum_tensor(f"up{i}", [P, CH], fp32)) for i in range(2)]
    add = [ctx.enter_context(nc.psum_tensor(f"add{i}", [P, 2, D], fp32)) for i in range(2)]
    resid = w["resid"]
    names = ["heads_in0", "heads_in1", "add_done", "added", "stats_done", "aggregated", "eps_added", "rstd_done", "normed",
             "transposed", "high", "low", "gate_done", "up_done", "silu_done", "prod_done", "mid_high", "mid_low", "stored"]
    g = {n: ctx.enter_context(nc.semaphore("l_" + n)) for n in names}

    work = [("wo", 0), ("wo", 1), ("up", 0), ("down", 0), ("up", 1), ("attn", 0), ("down", 1), ("up", 0), ("attn", 1),
            ("down", 0), ("up", 1), ("down", 1)]
    ADDS = TPC // 2
    parts_of = [KF if k == "up" else ADDS for k, _ in work]
    adders = [n for n, (k, _) in enumerate(work) if k != "up"]
    turners = [n for n, (k, _) in enumerate(work) if k != "down"]
    users = [n for n, (k, _) in enumerate(work) if k in ("up", "attn")]
    ups = [n for n, (k, _) in enumerate(work) if k == "up"]
    norm_no, turn_no, add_no, up_no = ({n: i for i, n in enumerate(x)} for x in (users, turners, adders, ups))

    def last_step(n, kinds):
        found = [m for m in range(n) if work[m][1] == work[n][1] and work[m][0] in kinds]
        return found[-1] if found else None

    events, norms = [("turn", 0)], []
    for n, (kind, i) in enumerate(work):
        for p in range(parts_of[n]):
            if p == parts_of[n] - (2 if kind == "up" else 1) and n + 1 in turn_no:
                if n + 1 in norms:
                    events.append(("norm", norms.pop(norms.index(n + 1))))
                events.append(("turn", n + 1))
            events.append(("part", n, p))
        if n in add_no:
            norms += [u for u in users if u > n and last_step(u, ("wo", "down", "attn")) == n]
        while norms and (norm_no[norms[0]] == 0 or ("turn", users[norm_no[norms[0]] - 1]) in events):
            events.append(("norm", norms.pop(0)))
    assert not norms
    assert [e[1] for e in events if e[0] == "norm"] == users and [e[1] for e in events if e[0] == "turn"] == turners

    def body(pair):
        def tile(i, t):
            return (pair * PAIR + i) * TPC + t

        def tiles(i, t, n):
            a = tile(i, t)
            return slice(a, a + n) if isinstance(pair, int) else bass.ds(a, n)

        with nc.Block() as block:
            @block.tensor
            def _(pe):
                def turn(n):
                    i, k0 = work[n][1], turn_no[n]
                    if n in norm_no:
                        pe.wait_ge(g["normed"], TPC * (norm_no[n] + 1))
                    else:
                        pe.wait_ge(g[f"heads_in{i}"], 1)
                    if k0:
                        pe.wait_ge(g["low"], k0)
                    for k in range(KD):
                        for t in range(TPC):
                            src = xh[:, t, P * k:P * k + P] if n in norm_no else heads[:, i, t, P * k:P * k + P]
                            last = nc.tensor.transpose(psT[:, k, P * t:P * t + P], src, c["ident"][:])
                    last.then_inc(g["transposed"], 1)

                def up_part(n, f):
                    i, u = work[n][1], KF * up_no[n] + f
                    if u >= 2:
                        pe.wait_ge(g["prod_done"], u - 1)
                    for which, banks, sem in ((1, gate, "gate_done"), (0, up, "up_done")):
                        steps = [(k, a, b) for k in range(KD) for a, b in PASSES]
                        for m, (k, a, b) in enumerate(steps):
                            at = INTER * which + P * f
                            last = nc.tensor.matmul(banks[u % 2][:], w["ug"][a][:, k, at:at + P], xT[i][b][:, k, :],
                                                    start=(m == 0), stop=(m == len(steps) - 1))
                        last.then_inc(g[sem], 1)

                def add_part(n, h):
                    kind, i = work[n]
                    left, right, kt = {"wo": (xT[i], w["wo"], KD), "down": (mid[i], w["dn"], KF),
                                       "attn": (xT[i], w["ab"], KD)}[kind]
                    r = ADDS * add_no[n] + h
                    if r >= 2:
                        pe.wait_ge(g["added"], r - 1)
                    for t in range(2):
                        at = P * (2 * h + t)
                        steps = [(k, a, b) for k in range(kt) for a, b in PASSES]
                        for m, (k, a, b) in enumerate(steps):
                            if kind == "down" and h == t == 0 and m % len(PASSES) == 0:
                                pe.wait_ge(g["mid_low"], KF * up_no[last_step(n, ("up",))] + k + 1)
                            last = nc.tensor.matmul(add[r % 2][:, t, :], left[a][:, k, at:at + P], right[b][:, k, :],
                                                    start=(m == 0), stop=(m == len(steps) - 1))
                    last.then_inc(g["add_done"], 1)

                for e in events:
                    if e[0] == "turn":
                        turn(e[1])
                    elif e[0] == "part":
                        if e[2] == 0 and e[1] in turn_no:
                            pe.wait_ge(g["low"], turn_no[e[1]] + 1)
                        (up_part if work[e[1]][0] == "up" else add_part)(e[1], e[2])

            @block.scalar
            def _(act):
                def high_part(n):
                    act.wait_ge(g["transposed"], turn_no[n] + 1)
                    before = last_step(n, ("wo", "up", "attn"))
                    if before is not None:
                        if work[before][0] == "up":
                            act.wait_ge(g["up_done"], KF * (up_no[before] + 1))
                        else:
                            act.wait_ge(g["add_done"], ADDS * (add_no[before] + 1))
                    nc.scalar.copy(xT[work[n][1]][0][:], psT[:]).then_inc(g["high"], 1)

                def high_mid(n, f):
                    u = KF * up_no[n] + f
                    act.wait_ge(g["prod_done"], u + 1)
                    nc.scalar.copy(mid[work[n][1]][0][:, f, :], prod[:, u % 2, :]).then_inc(g["mid_high"], 1)

                nc.scalar.copy(heads[:, 0, :, :], o_all[:, tiles(0, 0, TPC), :]).then_inc(g["heads_in0"], 1)
                for e in events:
                    if e[0] == "turn":
                        high_part(e[1])
                    elif e[0] == "part" and work[e[1]][0] == "up":
                        _, n, f = e
                        u = KF * up_no[n] + f
                        before = last_step(n, ("down",))
                        if f == 0 and before is not None:
                            act.wait_ge(g["add_done"], ADDS * (add_no[before] + 1))
                        act.wait_ge(g["gate_done"], u + 1)
                        if u >= 2:
                            act.wait_ge(g["prod_done"], u - 1)
                        nc.scalar.activation(silu[:, u % 2, :], gate[u % 2][:], ACT.Silu,
                                             scale=w["gain"][:, KF + f:KF + f + 1]).then_inc(g["silu_done"], 1)
                        if f:
                            high_mid(n, f - 1)
                        if f == KF - 1:
                            high_mid(n, f)

            @block.gpsimd
            def _(pool):
                nc.gpsimd.tensor_copy(heads[:, 1, :, :], o_all[:, tiles(1, 0, TPC), :]).then_inc(g["heads_in1"], 1)
                for e in events:
                    if e[0] == "norm":
                        k0 = norm_no[e[1]]
                        pool.wait_ge(g["aggregated"], TPC * (k0 + 1))
                        nc.gpsimd.tensor_scalar(rstd[:, :, 0], mv[:, :, 1], EPS, None, ALU.add).then_inc(g["eps_added"], 1)
                        pool.wait_ge(g["eps_added"], k0 + 1)
                        nc.gpsimd.tensor_tensor(rstd[:, :, 1], rstd[:, :, 0], c["rootexp"][:], ALU.pow).then_inc(g["rstd_done"], 1)
                    elif e[0] == "part" and work[e[1]][0] == "up":
                        i, f = work[e[1]][1], e[2]
                        u = KF * up_no[e[1]] + f
                        pool.wait_ge(g["mid_high"], u + 1)
                        nc.gpsimd.tensor_tensor(mid[i][1][:, f, :], prod[:, u % 2, :], mid[i][0][:, f, :].bitcast(fp32),
                                                ALU.subtract).then_inc(g["mid_low"], 1)

            @block.vector
            def _(dve):
                def norm(n):
                    k0, i = norm_no[n], work[n][1]
                    dve.wait_ge(g["added"], ADDS * (add_no[last_step(n, ("wo", "down", "attn"))] + 1))
                    if k0:
                        dve.wait_ge(g["normed"], TPC * k0)
                    for t in range(TPC):
                        nc.vector.bn_stats(stats[:, t, :], resid[:, tile(i, t), :]).then_inc(g["stats_done"], 1)
                    for t in range(TPC):
                        dve.wait_ge(g["stats_done"], TPC * k0 + t + 1)
                        nc.vector.bn_aggr(mv[:, t, :], stats[:, t, :]).then_inc(g["aggregated"], 1)
                    dve.wait_ge(g["rstd_done"], k0 + 1)
                    if k0:
                        dve.wait_ge(g["transposed"], turn_no[users[k0 - 1]] + 1)
                    for t in range(TPC):
                        nc.vector.tensor_scalar(xh[:, t, :], resid[:, tile(i, t), :], mv[:, t, 0:1],
                                                rstd[:, t, 1:2], ALU.subtract, ALU.mult).then_inc(g["normed"], 1)

                for e in events:
                    if e[0] == "norm":
                        norm(e[1])
                    elif e[0] == "turn":
                        dve.wait_ge(g["high"], turn_no[e[1]] + 1)
                        x = xT[work[e[1]][1]]
                        nc.vector.tensor_tensor(x[1][:], psT[:], x[0][:].bitcast(fp32), ALU.subtract).then_inc(g["low"], 1)
                    elif work[e[1]][0] == "up":
                        _, n, f = e
                        u = KF * up_no[n] + f
                        dve.wait_ge(g["silu_done"], u + 1)
                        dve.wait_ge(g["up_done"], u + 1)
                        if u >= 2:
                            dve.wait_ge(g["mid_low"], u - 1)
                        nc.vector.scalar_tensor_tensor(out=prod[:, u % 2, :], in0=up[u % 2][:], scalar=w["gain"][:, f:f + 1],
                                                       in1=silu[:, u % 2, :], op0=ALU.mult, op1=ALU.mult)\
                            .then_inc(g["prod_done"], 1)
                    else:
                        _, n, h = e
                        r = ADDS * add_no[n] + h
                        dve.wait_ge(g["add_done"], r + 1)
                        at = tiles(work[n][1], 2 * h, 2)
                        nc.vector.tensor_tensor(resid[:, at, :], resid[:, at, :], add[r % 2][:], ALU.add).then_inc(g["added"], 1)

            @block.sync
            def _(sp):
                for i in range(PAIR):
                    last = max(a for a in adders if work[a][1] == i)
                    sp.wait_ge(g["added"], ADDS * (add_no[last] + 1))
                    rows = out[0].rearrange("(t p) d -> p t d", p=P)
                    sp.dma_start(rows[:, tiles(i, 0, TPC), :], resid[:, tiles(i, 0, TPC), :]).then_inc(g["stored"], 16)
                sp.wait_ge(g["stored"], 16 * PAIR)
        clear(nc, list(g.values()))

    if loop:
        with nc.Fori(0, NCH // PAIR) as pair:
            body(pair)
    else:
        for pair in range(NCH // PAIR):
            body(pair)


def build(nc, x, w_q, w_k, w_v, w_o, weight_qkv, weight_out, SU_ug, SU_dp, Wscale_ug, Wscale_dp, W_up, W_gate, W_down, out,
          loop_layers=True):
    ins = dict(x=x, w_o=w_o, weight_qkv=weight_qkv, weight_out=weight_out, SU_ug=SU_ug, SU_dp=SU_dp,
               Wscale_ug=Wscale_ug, Wscale_dp=Wscale_dp, W_up=W_up, W_gate=W_gate, W_down=W_down)
    with ExitStack() as ctx:
        def sb(name, shape, dt=fp32, ctx=ctx):
            return ctx.enter_context(nc.sbuf_tensor(name, shape, dt))

        ident = sb("ident", [P, P])
        identb = sb("identb", [P, P], bf16)
        causal = sb("causal", [P, P], bf16)
        hadamard = sb("hadamard", [P, P])
        rootexp = sb("rootexp", [P, TPC])
        o_all = sb("o_all", [P, TILES, D])
        w = {n: sb(n, shape) for n, shape in (("gains", [P, 2 * KF]), ("gain", [P, 2 * KF]), ("su", [P, KD]), ("sud", [P, KF]),
                                              ("sdp", [P, D]))}
        base = nc.sbuf_base
        kept = [("resid", [P, TILES, D]), ("wo_raw", [P, KD, D])]
        made = [("ug", [P, KD, 2 * INTER]), ("dn", [P, KF, D]), ("ab", [P, KD, D]), ("wo", [P, KD, D])]
        raws = [("up_raw", [P, 2 * KF, D]), ("down_raw", [P, KD, INTER]), ("wv_raw", [P, KD, D]),
                ("wout_raw", [P, KD, D]), ("downT", [P, KF, D]), ("woutT", [P, KD, D])]

        def room(tensors):
            return sum(-(-4 * math.prod(shape[1:]) // 32) * 32 for _, shape in tensors)

        kept_at = base + 2 * room(made)
        raw_at = kept_at + room(kept)
        w.update(up_at=nc.sbuf_top - 4 * KD * 2 * INTER, raw_at=raw_at, raw_room=room(raws))
        for at, tensors in ((kept_at, kept), (raw_at, raws)):
            for i, (name, shape) in enumerate(tensors):
                w[name] = nc.alloc_sbuf_tensor_at(name, shape, fp32, offset=at + room(tensors[:i]))
        w["upT"] = nc.alloc_sbuf_tensor_at("upT", [P, KD, 2 * INTER], fp32, offset=w["up_at"])
        chunk_bytes, head_bytes = 2 * HEADS * CH, 2 * S
        assert kept_at >= base + (NCH - 1) * chunk_bytes and raw_at >= base + HEADS * head_bytes
        assert raw_at + room(raws) <= base + (HEADS + HEADS - GH) * head_bytes
        loaded = {n: ctx.enter_context(nc.semaphore("loaded_" + n)) for n in ("up", "down", "attn", "wo", "small", "resid")}
        with ExitStack() as attn:
            qs = sb("qs", [KM, NCH, HEADS, CH], bf16, attn)
            ks = sb("ks", [KM, HEADS, S], bf16, attn)
            v_aug = sb("v_aug", [P, TILES, HEADS, VW], fp32, attn)
            ones = o_all[:, TILES - 1, :].bitcast(bf16)
            stacked = [ctx.enter_context(nc.semaphore(f"stacked{c}")) for c in range(NCH)]
            stored = [ctx.enter_context(nc.semaphore(f"stored{i}")) for i in range(SLOTS)]
            scratch = nc.dram_tensor("qk_parts", (2, PARTS, D, S), bf16).ap()
            build_projections(nc, x, w_q, w_k, w_v, dict(ident=ident, identb=identb, causal=causal, hadamard=hadamard,
                                                         rootexp=rootexp, ones=ones),
                              qs, ks, v_aug, o_all, stacked, stored, scratch, lambda: load_vectors(nc, ins, w, loaded))
            build_attention(nc, attn, dict(qs=qs, ks=ks, v_aug=v_aug, o_all=o_all, ident=ident, identb=identb,
                                           causal=causal), stacked, stored, scratch,
                            later_loads(ins, w), loaded, w)
        c = dict(ident=ident, hadamard=hadamard, rootexp=rootexp)
        assert nc.sbuf_base == base
        for name, shape in made:
            w[name] = [sb(f"{name}{i}", shape, fp32r) for i in range(2)]
        assert nc.sbuf_base == kept_at
        sb("kept_room", [P, room(kept) // 4])
        build_weights(nc, c, w, loaded)
        with nc.Block() as block:
            @block.vector
            def _(dve):
                dve.wait_ge(loaded["resid"], 16 * NCH)
        build_layers(nc, ctx, ins, out, c, w, o_all, loop_layers)


_INS = ['L0_attn_a_x', 'L0_attn_a_w_q', 'L0_attn_a_w_k', 'L0_attn_a_w_v', 'L0_attn_a_w_o', 'L0_attn_b_weight_qkv',
        'L0_attn_b_weight_out', 'L0_ffn_SU_ug', 'L0_ffn_SU_dp', 'L0_ffn_Wscale_ug', 'L0_ffn_Wscale_dp', 'L0_ffn_W_up',
        'L0_ffn_W_gate', 'L0_ffn_W_down']


def kernel(**inputs):
    import numpy as _np
    import concourse.bacc as _bacc
    from concourse import mybir as _mybir
    from concourse.bass_utils import run_bass_kernel_spmd as _run

    nc = _bacc.Bacc("TRN2", target_bir_lowering=False, num_devices=1)
    arrays, args = {}, []
    for name in _INS:
        a = _np.ascontiguousarray(inputs[name])
        arrays[f"in_{name}_dram"] = a
        args.append(nc.dram_tensor(f"in_{name}_dram", a.shape, _mybir.dt.from_np(a.dtype), kind="ExternalInput").ap())
    out = nc.dram_tensor("out_0_dram", (1, S, D), fp32, kind="ExternalOutput").ap()
    build(nc, *args, out)
    r = _run(nc, [arrays], core_ids=[0])
    return r.results[0]["out_0_dram"]
```

```python
import concourse.bass as bass
from concourse import mybir
from contextlib import ExitStack
import math

fp32 = mybir.dt.float32
fp32r = mybir.dt.float32r
bf16 = mybir.dt.bfloat16
ALU = mybir.AluOpType
ACT = mybir.ActivationFunctionType
AX = mybir.AxisListType

P = 128
S = 2048
D = 256
KD = D // P
HEADS = 16
DH = D // HEADS
INTER = 1024
KF = INTER // P
CH = 512
NCH = S // CH
TPC = CH // P
TILES = S // P
GH = 4
NG = HEADS // GH
EPS = 1e-5
MASKED = -3.0e38
PARTS = 3
Q_PARTS = (0, 1, 2, 0, 1, 0)
K_PARTS = (2, 1, 0, 1, 0, 0)
Q_RUNS = ((0, 0, 3), (3, 0, 2), (5, 0, 1))
K_RUNS = ((0, 0, 3), (3, 1, 2), (5, 2, 1))
assert Q_PARTS == tuple(p for _, first, n in Q_RUNS for p in range(first, first + n))
assert K_PARTS == tuple(PARTS - 1 - p for _, first, n in K_RUNS for p in range(first, first + n))
KS = len(Q_PARTS) * DH
KM = KS + 2
VW = DH + 1
STACK_IN = 16 * 2 * len(Q_RUNS)
PASSES = ((0, 0), (0, 1), (1, 0))


def clear(nc, sems):
    nc.all_engine_barrier()
    for s in sems:
        nc.gpsimd.sem_clear(s)
    nc.all_engine_barrier()


def build_constants(nc, ident, identb, causal, ones, rootexp, first_loads):
    with ExitStack() as ctx:
        filled = ctx.enter_context(nc.semaphore("c_filled"))
        ready = ctx.enter_context(nc.semaphore("c_ready"))
        with nc.Block() as block:
            @block.gpsimd
            def _(pool):
                nc.gpsimd.memset(ident[:], 0.0).then_inc(filled, 1)
                nc.gpsimd.memset(identb[:], 0.0).then_inc(filled, 1)
                nc.gpsimd.memset(causal[:], 0.0).then_inc(filled, 1)
                nc.gpsimd.memset(ones[:], 1.0).then_inc(filled, 1)
                nc.gpsimd.memset(rootexp[:], -0.5).then_inc(filled, 1)
                pool.wait_ge(filled, 5)
                nc.gpsimd.affine_select(out=ident[:], in_=ident[:], compare_op=ALU.not_equal, fill=1.0, base=0,
                                        pattern=[[-1, P]], channel_multiplier=1).then_inc(ready, 1)
                nc.gpsimd.affine_select(out=identb[:], in_=identb[:], compare_op=ALU.not_equal, fill=1.0, base=0,
                                        pattern=[[-1, P]], channel_multiplier=1).then_inc(ready, 1)
                nc.gpsimd.affine_select(out=causal[:], in_=causal[:], compare_op=ALU.is_ge, fill=MASKED, base=0,
                                        pattern=[[-1, P]], channel_multiplier=1).then_inc(ready, 1)

            @block.sync
            def _(_):
                first_loads()
        clear(nc, (filled, ready))


NU = 2 * KD
SLOTS = 7
OWN_SLOTS = (0, 1, 3, 5, 6)
LENT_SLOTS = tuple(n for n in range(SLOTS) if n not in OWN_SLOTS)
SENT_EARLY = 12


def send(engine, n, parts, scratch, stored):
    c, u = divmod(n, NU)
    engine.dma_start(scratch[u // KD, :, P * (u % KD):P * (u % KD) + P, CH * c:CH * c + CH].rearrange("a p n -> p a n"),
                     parts(n)).then_inc(stored[n % SLOTS], 16)


def load_stack(sp, m, qs, ks, scratch, stored, stacked):
    c, u = divmod(m, NU)
    for i in range(KD):
        sp.wait_ge(stored[(m + i) % SLOTS], 16 * ((m + i) // SLOTS + 1))
    if m == NU * (NCH - 1):
        for slot in LENT_SLOTS:
            sp.wait_ge(stored[slot], 16 * len(range(slot, NU * NCH, SLOTS)))
    for block0, part0, n in Q_RUNS if u < KD else K_RUNS:
        rows = slice(DH * block0, DH * (block0 + n))
        sp.dma_start(qs[rows, c, :, :] if u < KD else ks[rows, :, CH * c:CH * c + CH],
                     scratch[u // KD, part0:part0 + n, :, CH * c:CH * c + CH]
                     .rearrange("a (d h) n -> (a d) h n", d=DH)).then_inc(stacked[c], 16)


def build_projections(nc, x, w_q, w_k, w_v, c0, qs, ks, v_aug, parts, spare_xT, stacked, stored, scratch, load_vectors):
    ident, rootexp, ones = c0["ident"], c0["rootexp"], c0["ones"]
    UNITS = NU + TPC // 2
    with ExitStack() as ctx:
        def sb(name, shape, dt=fp32):
            return ctx.enter_context(nc.sbuf_tensor(name, shape, dt))

        xin = sb("xin", [P, 2, TPC, D])
        wraw = sb("wraw", [P, 3, KD, D])
        rest = sb("rest", [P, 2, CH])
        xT = [[sb(f"xT{i}", [P, KD, CH], fp32r) for i in range(2)], spare_xT]
        wsp = [sb(f"wsp{i}", [P, 3, KD, D], fp32r) for i in range(2)]
        stats = sb("stats1", [P, TPC, 6])
        mv = sb("mv1", [P, TPC, 2])
        rstd = sb("rstd1", [P, TPC, 2])
        psT = ctx.enter_context(nc.psum_tensor("psT1", [P, KD, CH], fp32))
        unit = [ctx.enter_context(nc.psum_tensor(f"unit{i}", [P, CH], fp32)) for i in range(UNITS)]

        names = ["x_in0", "x_in1", "w_in0", "w_in1", "w_in2", "w_high", "w_low", "stats_done", "aggregated", "eps_added", "rstd_done",
                 "normed", "transposed", "high_done", "low_done", "unit_done", "part1_done", "rest_done",
                 "part2_done", "parts_done", "v_done", "ones_in", "v_ones"]
        sems = {n: ctx.enter_context(nc.semaphore("p_" + n)) for n in names}
        x_in = (sems["x_in0"], sems["x_in1"])
        g = sems

        def load_x(engine, c):
            engine.dma_start(xin[:, c % 2, :, :],
                             x[0, CH * c:CH * c + CH, :].rearrange("(t p) d -> p t d", p=P)).then_inc(x_in[c % 2], 16)

        def first_loads():
            load_x(nc.sync, 0)
            for n, w in enumerate((w_q, w_k, w_v)):
                nc.sync.dma_start(wraw[:, n, :, :], w.rearrange("(k p) n -> p k n", p=P)).then_inc(g[f"w_in{n}"], 16)
            load_x(nc.sync, 1)
            load_vectors()

        build_constants(nc, ident, c0["identb"], c0["causal"], ones, rootexp, first_loads)
        with nc.Block() as block:
            @block.sync
            def _(sp):
                for r in range(2):
                    sp.dma_start(ks[KS + r:KS + r + 1, :, :].rearrange("p h (b n) -> p (h b) n", n=CH),
                                 ones[64 * r:64 * r + 64, :]).then_inc(g["ones_in"], 16)
                for n in range(SENT_EARLY):
                    if n % KD == 1 and n >= 3:
                        load_stack(sp, n - 3, qs, ks, scratch, stored, stacked)
                    sp.wait_ge(g["parts_done"], n + 1)
                    send(sp, n, parts, scratch, stored)
                sp.wait_ge(g["ones_in"], 32)

            def weight(n):
                views = [w[:, n, :, :] for w in (wraw, wsp[0], wsp[1])]
                if n == 2:
                    return views
                return [views[0].rearrange("p k (h d) -> p k d h", d=DH)] + [v.rearrange("p k (d h) -> p k d h", d=DH) for v in views[1:]]

            def lie(n, part):
                return part if n % NU < KD else PARTS - 1 - part

            def second_part(act, n):
                act.wait_ge(g["rest_done"], n + 1)
                nc.scalar.copy(parts(n)[:, lie(n, 1), :], rest[:, n % 2, :]).then_inc(g["part2_done"], 1)

            def high_part(act, c):
                act.wait_ge(g["transposed"], c + 1)
                if c >= 2:
                    act.wait_ge(g["unit_done"], UNITS * (c - 1))
                nc.scalar.copy(xT[c % 2][0][:], psT[:]).then_inc(g["high_done"], 1)
                if c + 2 < NCH:
                    load_x(act, c + 2)

            def chunk(act, c):
                for u in range(UNITS):
                    act.wait_ge(g["unit_done"], UNITS * c + u + 1)
                    if u and u <= NU:
                        second_part(act, NU * c + u - 1)
                    if u < NU:
                        n = NU * c + u
                        if n >= SLOTS:
                            act.wait_ge(stored[n % SLOTS], 16 * (n // SLOTS))
                        nc.scalar.copy(parts(n)[:, lie(n, 0), :], unit[u][:]).then_inc(g["part1_done"], 1)
                        if u == 2 and c + 1 < NCH:
                            high_part(act, c + 1)
                    else:
                        if c == 0:
                            act.wait_ge(g["v_ones"], 1)
                        t = TPC * c + 2 * (u - NU)
                        nc.scalar.copy(v_aug[:, t:t + 2, :, 0:DH],
                                       unit[u][:].rearrange("p (t h d) -> p t h d", t=2, d=DH)).then_inc(g["v_done"], 1)

            @block.scalar
            def _(act):
                for n in range(3):
                    raw, high, _ = weight(n)
                    act.wait_ge(g[f"w_in{n}"], 16)
                    nc.scalar.copy(high, raw).then_inc(g["w_high"], 1)
                high_part(act, 0)
                for c in range(NCH):
                    chunk(act, c)

            @block.gpsimd
            def _(pool):
                nc.gpsimd.memset(v_aug[:, :, :, DH:VW], 1.0).then_inc(g["v_ones"], 1)

                def root(c):
                    pool.wait_ge(g["aggregated"], TPC * (c + 1))
                    nc.gpsimd.tensor_scalar(rstd[:, :, 0], mv[:, :, 1], EPS, None, ALU.add).then_inc(g["eps_added"], 1)
                    pool.wait_ge(g["eps_added"], c + 1)
                    nc.gpsimd.tensor_tensor(rstd[:, :, 1], rstd[:, :, 0], rootexp[:], ALU.pow).then_inc(g["rstd_done"], 1)

                root(0)
                for c in range(NCH):
                    if c + 1 < NCH:
                        root(c + 1)
                    for u in range(NU):
                        n = NU * c + u
                        pool.wait_ge(g["part2_done"], n + 1)
                        nc.gpsimd.tensor_tensor(parts(n)[:, lie(n, 2), :], rest[:, n % 2, :], parts(n)[:, lie(n, 1), :],
                                                ALU.subtract).then_inc(g["parts_done"], 1)

            @block.vector
            def _(dve):
                def statistics(c):
                    dve.wait_ge(x_in[c % 2], 16 * (c // 2 + 1))
                    if c:
                        dve.wait_ge(g["normed"], TPC * c)
                    for t in range(TPC):
                        nc.vector.bn_stats(stats[:, t, :], xin[:, c % 2, t, :]).then_inc(g["stats_done"], 1)
                    for t in range(TPC):
                        dve.wait_ge(g["stats_done"], TPC * c + t + 1)
                        nc.vector.bn_aggr(mv[:, t, :], stats[:, t, :]).then_inc(g["aggregated"], 1)

                def normalise(c):
                    dve.wait_ge(g["rstd_done"], c + 1)
                    for t in range(TPC):
                        nc.vector.tensor_scalar(xin[:, c % 2, t, :], xin[:, c % 2, t, :], mv[:, t, 0:1],
                                                rstd[:, t, 1:2], ALU.subtract, ALU.mult).then_inc(g["normed"], 1)

                def low_weight(n):
                    raw, high, low = weight(n)
                    dve.wait_ge(g["w_high"], n + 1)
                    nc.vector.tensor_tensor(low, raw, high.bitcast(fp32), ALU.subtract).then_inc(g["w_low"], 1)

                statistics(0)
                low_weight(0)
                normalise(0)
                low_weight(1)
                low_weight(2)
                def low_part(c):
                    dve.wait_ge(g["high_done"], c + 1)
                    nc.vector.tensor_tensor(xT[c % 2][1][:], psT[:], xT[c % 2][0][:].bitcast(fp32), ALU.subtract).then_inc(g["low_done"], 1)

                statistics(1)
                low_part(0)
                for c in range(NCH):
                    for u in range(NU):
                        n = NU * c + u
                        dve.wait_ge(g["part1_done"], n + 1)
                        if n >= 2:
                            dve.wait_ge(g["parts_done"], n - 1)
                        nc.vector.tensor_tensor(rest[:, n % 2, :], unit[u][:], parts(n)[:, lie(n, 0), :],
                                                ALU.subtract).then_inc(g["rest_done"], 1)
                        if u == 0 and c + 1 < NCH:
                            normalise(c + 1)
                        if u == 2 and c + 1 < NCH:
                            low_part(c + 1)
                        if u == 2 and c + 2 < NCH:
                            statistics(c + 2)

            @block.tensor
            def _(pe):
                def transposes(c):
                    pe.wait_ge(g["normed"], TPC * (c + 1))
                    if c:
                        pe.wait_ge(g["low_done"], c)
                    for k in range(KD):
                        for t in range(TPC):
                            last = nc.tensor.transpose(psT[:, k, P * t:P * t + P], xin[:, c % 2, t, P * k:P * k + P], ident[:])
                    last.then_inc(g["transposed"], 1)

                transposes(0)
                for c in range(NCH):
                    pe.wait_ge(g["low_done"], c + 1)
                    for u in range(UNITS):
                        if c == 0 and (u == NU or u < NU and u % KD == 0):
                            pe.wait_ge(g["w_low"], u // KD + 1)
                        if c and u < NU:
                            pe.wait_ge(g["rest_done"], NU * (c - 1) + u + 1)
                        if c and u >= NU:
                            pe.wait_ge(g["v_done"], (UNITS - NU) * (c - 1) + u - NU + 1)
                        steps = [(k, a, b) for k in range(KD) for a, b in PASSES]
                        if u < NU:
                            m = u % KD
                            for i, (k, a, b) in enumerate(steps):
                                last = nc.tensor.matmul(unit[u][:], wsp[a][:, u // KD, k, P * m:P * m + P], xT[c % 2][b][:, k, :],
                                                        start=(i == 0), stop=(i == len(steps) - 1))
                        else:
                            for t in range(2):
                                at = P * (2 * (u - NU) + t)
                                for i, (k, a, b) in enumerate(steps):
                                    last = nc.tensor.matmul(unit[u][:, D * t:D * t + D], xT[c % 2][a][:, k, at:at + P], wsp[b][:, 2, k, :],
                                                            start=(i == 0), stop=(i == len(steps) - 1))
                        last.then_inc(g["unit_done"], 1)
                        if u == 1 and c + 1 < NCH:
                            transposes(c + 1)
        clear(nc, list(sems.values()))


ITEMS = [(group, c) for group in range(NG) for c in (range(NCH) if group < NG - 1 else reversed(range(NCH)))]
PIECES = [(i, qb, j, k0, min(CH, P * (qb + 1) - k0)) for i, (_, c) in enumerate(ITEMS)
          for qb in range(TPC * c, TPC * c + TPC) for j in range(GH) for k0 in range(0, P * (qb + 1), CH)]
QUADS = [(i, kb, P * max(0, kb - TPC * c), CH - P * max(0, kb - TPC * c))
         for i, (_, c) in enumerate(ITEMS) for kb in range(TPC * (c + 1))]
LAST_QUAD = {q[0]: n for n, q in enumerate(QUADS)}
LAST_PIECE = {p[0]: n for n, p in enumerate(PIECES)}
FIRST_PIECE = {p[0]: n for n, p in reversed(list(enumerate(PIECES)))}
ST_BANKS = 3
MAX_BANKS = 4
P_SLOTS = 12
ROWS_IN = 16 * 2
TURNS = [("down", f, 0) for f in range(0, KF, 2)] + [("up", f, k) for k in range(KD) for f in range(0, 2 * KF, 4)]
TURNS += [("out", 0, 0)]
LEAD = 64 * CH


def plan():
    hop, act_wait, act_col, dve_wait, dve_col, rows_in = 200.0, 50.0, 1 / 1.2, 65.0, 1 / 0.96, 4500.0
    work = []
    for n, p in enumerate(PIECES):
        if p[0] and n == FIRST_PIECE[p[0]] + 3:
            work.append(("T", p[0] - 1))
        work.append(("M", n))
    work.append(("T", len(ITEMS) - 1))
    work.reverse()
    pe = act = dve = pool = 0.0
    exp_at, rows_at, maxima_at, read_at, scaled_at = {}, {}, {}, {}, {}
    st_free, max_free, turns, order = [], [], [], []
    s = v = w = done = seen = 0
    while s < GH * len(QUADS) or work or v < len(QUADS) or turns or w < len(TURNS):
        can = {}
        if s < GH * len(QUADS) and (s < P_SLOTS or GH * v > s - P_SLOTS):
            i, kb, _, nq = QUADS[s // GH]
            if i in rows_at:
                can["S"] = max(pe, rows_at[i] if kb == 0 else 0, st_free[-ST_BANKS] if len(st_free) >= ST_BANKS else 0)
        if work:
            kind, n = work[-1]
            waiting = s < GH * len(QUADS) and QUADS[s // GH][0] not in rows_at
            if kind == "T" or done < seen + LEAD or waiting or s == GH * len(QUADS):
                can[kind] = max(pe, max_free[-MAX_BANKS] if len(max_free) >= MAX_BANKS else 0,
                                maxima_at[n] if kind == "T" else 0)
        if v < len(QUADS) and s >= GH * (v + 1):
            i, kb, _, nq = QUADS[v]
            if kb or not i or i - 1 in read_at:
                can["V"] = max(pe, exp_at[v], read_at[i - 1] if kb == 0 and i else 0)
        if turns:
            can["R"] = max(pe, st_free[-ST_BANKS], read_at[turns[0]])
        if not work and w < len(TURNS) and v >= LAST_QUAD[len(ITEMS) - GH]:
            can["W"] = max(pe, max_free[-MAX_BANKS])
        now = min(can.values())
        ready = [k for k in ("T", "R", "S", "M", "V", "W") if k in can and can[k] <= now + 1]
        act_left, dve_left = act - pe, dve - pe
        if ready[0] in "TR":
            kind = ready[0]
        elif "S" in ready and act_left < 100 and not ("M" in ready and dve_left < act_left):
            kind = "S"
        elif "M" in ready and dve_left < 100:
            kind = "M"
        elif "V" in ready and (ready[0] == "V" or (act_left > 1200 and (dve_left > 1500 or not work))):
            kind = "V"
        elif "S" in ready and "M" in ready:
            kind = "S" if act_left <= dve_left else "M"
        else:
            kind = ready[0]
        pe = now
        if kind == "S":
            i, kb, _, nq = QUADS[s // GH]
            pe += nq / 2.4
            act = max(act, pe + hop) + act_wait + act_col * nq
            st_free.append(act + hop)
            exp_at[s // GH] = act + hop
            if kb >= TPC * ITEMS[i][1]:
                pool = max(pool, act + hop) + 244
                exp_at[s // GH] = pool + hop
            order.append(("S", s // GH, s % GH))
            s, seen = s + 1, seen + nq
        elif kind == "M":
            n = work.pop()[1]
            i, _, _, _, nk = PIECES[n]
            pe += nk / 2.4
            dve = max(dve, pe + hop) + dve_wait + dve_col * nk
            max_free.append(dve + hop)
            done += nk
            if LAST_PIECE[i] == n:
                dve += 800
                maxima_at[i] = dve + hop
            order.append(("M", n))
        elif kind == "T":
            i = work.pop()[1]
            pe += 60
            dve = max(dve, pe + hop) + 2 * dve_wait
            max_free.append(dve + hop)
            rows_at[i] = dve + rows_in
            order.append(("T", i))
        elif kind == "W":
            pe += 4 * 4 * P / 2.4
            dve = max(dve, pe + hop) + dve_wait + dve_col * CH
            max_free.append(dve + hop)
            order.append(("W", w))
            w += 1
        elif kind == "V":
            i, _, _, nq = QUADS[v]
            pe += 2 * nq / 1.2 + 60
            if LAST_QUAD[i] == v:
                act = max(act, pe + hop, scaled_at.get(i - 1, 0)) + act_wait + act_col * CH
                read_at[i] = act + hop
                turns.append(i)
            order.append(("V", v))
            v += 1
        else:
            i = turns.pop(0)
            pe += 440
            dve = max(dve, pe + hop) + 700
            scaled_at[i] = dve + hop
            st_free.append(dve + hop)
            order.append(("R", i))
    return order


def later_loads(ins, w):
    up, down, resid = w["up_raw"], w["down_raw"], w["resid"]
    half = KF // 2
    loads = []
    for name, at in (("W_up", 0), ("W_gate", KF)):
        rows = ins[name].rearrange("(f p) j -> p f j", p=P)
        loads += [(up[:, at + f:at + f + half, :], rows[:, f:f + half, :], "up") for f in (0, half)]
    rows = ins["W_down"].rearrange("(k p) j -> p k j", p=P)
    loads += [(down[:, k, :], rows[:, k, :], "down") for k in range(KD)]
    loads += [(w["wv_raw"][:], ins["weight_qkv"][2 * D:3 * D, :].rearrange("(k p) j -> p k j", p=P), "attn"),
              (w["wout_raw"][:], ins["weight_out"].rearrange("(k p) j -> p k j", p=P), "attn"),
              (w["wo_raw"][:], ins["w_o"].rearrange("(k p) n -> p k n", p=P), "wo")]
    rows = ins["x"][0].rearrange("(t p) d -> p t d", p=P)
    return loads + [(resid[:, t:t + TPC, :], rows[:, t:t + TPC, :], "resid") for t in range(0, TILES, TPC)]


def load_vectors(nc, ins, w, loaded):
    with nc.allow_non_contiguous_dma(reason="single numbers, few"):
        for name, src in (("su", "SU_ug"), ("sud", "SU_dp"), ("gains", "Wscale_ug")):
            nc.sync.dma_start(w[name][:], ins[src].rearrange("(k p) -> p k", p=P)).then_inc(loaded["small"], 16)
    nc.sync.dma_start(w["sdp"][:], ins["Wscale_dp"].rearrange("(a n) -> a n", a=1).to_broadcast([P, D])).then_inc(loaded["small"], 16)


def build_attention(nc, ctx, t, stacked, stored, scratch, loads, loaded, w):
    def sb(name, shape, dt=fp32):
        return ctx.enter_context(nc.sbuf_tensor(name, shape, dt))

    qs, ks, v_aug, o_all = t["qs"], t["ks"], t["v_aug"], t["o_all"]
    ident, identb, causal, hadamard = t["ident"], t["identb"], t["causal"], t["hadamard"]
    mx = sb("mx", [P, GH, TPC, NCH])
    mtmp = sb("mtmp", [P, GH, TPC])
    mparts = sb("mparts", [P, 2 * GH * TPC], bf16)
    tmp = sb("had_tmp", [P, P])
    mrow = sb("mrow", [32, P], bf16)
    probs = sb("probs", [P, P_SLOTS, CH])
    oraw = sb("oraw", [P, CH])
    rec = sb("rec", [P, TPC, GH])
    smax = [ctx.enter_context(nc.psum_tensor(f"smax{i}", [P, CH], fp32)) for i in range(MAX_BANKS)]
    st = [ctx.enter_context(nc.psum_tensor(f"st{i}", [P, CH], fp32)) for i in range(ST_BANKS)]
    ops = ctx.enter_context(nc.psum_tensor("ops", [P, CH], fp32))
    names = ["smax_done", "smax_read", "mparts_done", "max_row", "score_done", "exp_done", "masked", "pv_done", "o_read",
             "turned", "inverted", "scaled", "combined", "zeroed", "level"]
    g = {n: ctx.enter_context(nc.semaphore("a_" + n)) for n in names}

    assert nc.sbuf_base <= w["up_at"]
    order = plan()
    smax_at = {o: n for n, o in enumerate(o for o in order if o[0] in "MTW")}
    st_at = {o: n for n, o in enumerate(o for o in order if o[0] in "SR")}
    frees, exps, divides = [], 0, 0
    for o in st_at:
        if o[0] == "S":
            exps += 1
            frees.append(("exp_done", exps))
        else:
            divides += 1
            frees.append(("scaled", divides))
    diag = [kb >= TPC * ITEMS[i][1] for i, kb, _, _ in QUADS]
    masks_before = [GH * sum(diag[:n]) for n in range(len(QUADS) + 1)]

    with nc.Block() as block:
        @block.tensor
        def _(pe):
            pe.wait_ge(g["zeroed"], 1)
            nc.tensor.matmul(ops[:], probs[:, 0, 0:P], probs[:, 0, :], start=True, stop=True)
            for o in order:
                if o[0] in "MTW":
                    n = smax_at[o]
                    bank = smax[n % MAX_BANKS]
                    if n >= MAX_BANKS:
                        pe.wait_ge(g["smax_read"], n - MAX_BANKS + 1)
                    if o[0] == "M":
                        i, qb, j, k0, nk = PIECES[o[1]]
                        group, c = ITEMS[i]
                        if group == 0 and o[1] == FIRST_PIECE[i]:
                            pe.wait_ge(stacked[c], STACK_IN)
                        masked = k0 + nk == P * (qb + 1)
                        last = nc.tensor.matmul(bank[:, 0:nk], qs[0:KS, c, GH * group + j, P * (qb % TPC):P * (qb % TPC) + P],
                                                ks[0:KS, GH * group + j, k0:k0 + nk], start=True, stop=not masked)
                        if masked:
                            last = nc.tensor.matmul(bank[:, nk - P:nk], identb[:], causal[:], start=False, stop=True)
                    elif o[0] == "W":
                        kind, f, k = TURNS[o[1]]
                        if kind == "up":
                            pe.wait_ge(loaded["up"], 64)
                            blocks = [w["up_raw"][:, f + i, P * k:P * k + P] for i in range(4)]
                        elif kind == "down":
                            pe.wait_ge(loaded["down"], 32)
                            blocks = [w["down_raw"][:, j, P * (f + i):P * (f + i) + P] for i in range(2) for j in range(KD)]
                        else:
                            pe.wait_ge(loaded["attn"], 32)
                            blocks = [w["wout_raw"][:, j, P * i:P * i + P] for i in range(KD) for j in range(KD)]
                        for i, block_in in enumerate(blocks):
                            last = nc.tensor.transpose(bank[:, P * i:P * i + P], block_in, ident[:])
                    else:
                        pe.wait_ge(g["mparts_done"], o[1] + 1)
                        last = nc.tensor.transpose(bank[0:32, 0:P // 2].bitcast(bf16), mparts[:], identb[:])
                    last.then_inc(g["smax_done"], 1)
                elif o[0] == "S":
                    _, n, j = o
                    i, kb, q0, nq = QUADS[n]
                    group, c = ITEMS[i]
                    use = st_at[o]
                    if use >= ST_BANKS:
                        pe.wait_ge(g[frees[use - ST_BANKS][0]], frees[use - ST_BANKS][1])
                    if j == 0 and kb == 0:
                        pe.wait_ge(g["max_row"], ROWS_IN * (i + 1))
                    head = GH * group + j
                    nc.tensor.matmul(st[use % ST_BANKS][:, 0:nq], ks[0:KM, head, P * kb:P * kb + P],
                                     qs[0:KM, c, head, q0:CH], start=True, stop=True).then_inc(g["score_done"], 1)
                elif o[0] == "V":
                    n = o[1]
                    i, kb, q0, nq = QUADS[n]
                    group, c = ITEMS[i]
                    if kb == 0 and i:
                        pe.wait_ge(g["o_read"], i)
                    pe.wait_ge(g["exp_done"], GH * (n + 1))
                    if diag[n]:
                        pe.wait_ge(g["masked"], masks_before[n + 1])
                    for j in range(GH):
                        u = GH * n + j
                        nc.tensor.matmul(ops[32 * j:32 * j + VW, q0:CH], v_aug[:, kb, GH * group + j, :],
                                         probs[:, u % P_SLOTS, 0:nq],
                                         start=(kb == 0), stop=(kb == TPC * (c + 1) - 1)).then_inc(g["pv_done"], 1)
                else:
                    use = st_at[o]
                    pe.wait_ge(g[frees[use - ST_BANKS][0]], frees[use - ST_BANKS][1])
                    pe.wait_ge(g["o_read"], o[1] + 1)
                    for b in range(TPC):
                        last = nc.tensor.transpose(st[use % ST_BANKS][:, P * b:P * b + P], oraw[:, P * b:P * b + P], ident[:])
                    last.then_inc(g["turned"], 1)

        @block.scalar
        def _(act):
            for n in range(SENT_EARLY, NU * NCH):
                if n % KD == 1 and n < NU * NCH - 1:
                    load_stack(act, n - 3, qs, ks, scratch, stored, stacked)
                send(act, n, t["parts"], scratch, stored)
            later = list(loads)
            for o in order:
                if o[0] == "S":
                    _, n, j = o
                    i, kb, q0, nq = QUADS[n]
                    group = ITEMS[i][0]
                    u = GH * n + j
                    act.wait_ge(g["score_done"], u + 1)
                    if group == NG - 1 and j == 0 and later and (later[0][2] not in ("wo", "resid") or ITEMS[i][1] < NCH - 1):
                        dst, src, name = later.pop(0)
                        act.dma_start(dst, src).then_inc(loaded[name], 16)
                    if u >= P_SLOTS:
                        act.wait_ge(g["pv_done"], u - P_SLOTS + 1)
                    nc.scalar.activation(probs[:, u % P_SLOTS, 0:nq], st[st_at[o] % ST_BANKS][:, 0:nq], ACT.Exp,
                                         scale=DH ** -0.5).then_inc(g["exp_done"], 1)
                elif o[0] == "V" and LAST_QUAD[QUADS[o[1]][0]] == o[1]:
                    i = QUADS[o[1]][0]
                    act.wait_ge(g["pv_done"], GH * (o[1] + 1))
                    if i:
                        act.wait_ge(g["scaled"], i)
                    nc.scalar.copy(oraw[:], ops[:]).then_inc(g["o_read"], 1)

        @block.vector
        def _(dve):
            def hadamard_levels():
                src, n, width = ident, 0, 1
                while width < P:
                    dst = hadamard if src is not hadamard else tmp
                    a = src[:].rearrange("p (a two h) -> p a two h", two=2, h=width)
                    b = dst[:].rearrange("p (a two h) -> p a two h", two=2, h=width)
                    if n:
                        dve.wait_ge(g["level"], n)
                    nc.vector.tensor_tensor(b[:, :, 0, :], a[:, :, 0, :], a[:, :, 1, :], ALU.add).then_inc(g["level"], 1)
                    nc.vector.tensor_tensor(b[:, :, 1, :], a[:, :, 0, :], a[:, :, 1, :], ALU.subtract).then_inc(g["level"], 1)
                    src, n, width = dst, n + 2, 2 * width
                assert src is hadamard

            nc.vector.memset(probs[:, 0, :], 0.0).then_inc(g["zeroed"], 1)
            reads = 0
            combined = 0
            for o in order:
                if o[0] == "M":
                    i, qb, j, k0, nk = PIECES[o[1]]
                    c = ITEMS[i][1]
                    n = smax_at[o]
                    if i and o[1] == FIRST_PIECE[i]:
                        dve.wait_ge(g["mparts_done"], i)
                    dve.wait_ge(g["smax_done"], n + 1)
                    nc.vector.reduce_max(mx[:, j, qb % TPC, k0 // CH:k0 // CH + 1], smax[n % MAX_BANKS][:, 0:nk], AX.X)\
                        .then_inc(g["smax_read"], 1)
                    reads += 1
                    if o[1] == LAST_PIECE[i]:
                        dve.wait_ge(g["smax_read"], reads)
                        high = mparts[:, 0:GH * TPC].rearrange("p (j q) -> p j q", j=GH)
                        low = mparts[:, GH * TPC:2 * GH * TPC].rearrange("p (j q) -> p j q", j=GH)
                        m = mx[:, :, :, 0]
                        if c:
                            nc.vector.reduce_max(mtmp[:], mx[:, :, :, 0:c + 1], AX.X).then_inc(g["combined"], 1)
                            combined += 1
                            dve.wait_ge(g["combined"], combined)
                            m = mtmp[:]
                        nc.vector.tensor_scalar(high, m, -1.0, None, ALU.mult).then_inc(g["combined"], 1)
                        combined += 1
                        dve.wait_ge(g["combined"], combined)
                        nc.vector.scalar_tensor_tensor(out=low, in0=m, scalar=-1.0, in1=high, op0=ALU.mult,
                                                       op1=ALU.subtract).then_inc(g["mparts_done"], 1)
                elif o[0] == "W":
                    if o[1] == 0:
                        hadamard_levels()
                    kind, f, k = TURNS[o[1]]
                    n = smax_at[o]
                    if kind == "up":
                        dst = w["upT"][:, k, P * f:P * f + CH]
                    else:
                        dst = w["downT"][:, f:f + 2, :] if kind == "down" else w["woutT"][:]
                    dve.wait_ge(g["smax_done"], n + 1)
                    nc.vector.tensor_copy(dst, _like(smax[n % MAX_BANKS][:], dst)).then_inc(g["smax_read"], 1)
                    reads += 1
                elif o[0] == "T":
                    n = smax_at[o]
                    dve.wait_ge(g["smax_done"], n + 1)
                    if o[1]:
                        dve.wait_ge(g["max_row"], ROWS_IN * o[1])
                    nc.vector.tensor_copy(mrow[:], smax[n % MAX_BANKS][0:32, 0:P // 2].bitcast(bf16)).then_inc(g["smax_read"], 1)
                    reads += 1
                elif o[0] == "R":
                    i = o[1]
                    group, c = ITEMS[i]
                    sums = st[st_at[o] % ST_BANKS][:].rearrange("p (t j d) -> p t j d", t=TPC, j=GH)
                    dve.wait_ge(g["turned"], i + 1)
                    if i:
                        dve.wait_ge(g["scaled"], i)
                    else:
                        for slot in range(SLOTS):
                            dve.wait_ge(stored[slot], 16 * len(range(slot, NU * NCH, SLOTS)))
                    nc.vector.reciprocal(rec[:], sums[:, :, :, DH]).then_inc(g["inverted"], 1)
                    dve.wait_ge(g["inverted"], i + 1)
                    dst = o_all[:, TPC * c:TPC * c + TPC, GH * DH * group:GH * DH * group + GH * DH]
                    nc.vector.tensor_tensor(dst.rearrange("p t (j d) -> p t j d", j=GH), sums[:, :, :, 0:DH],
                                            rec[:].unsqueeze(3).to_broadcast([P, TPC, GH, DH]), ALU.mult).then_inc(g["scaled"], 1)

        @block.gpsimd
        def _(pool):
            for n, (i, kb, q0, nq) in enumerate(QUADS):
                if diag[n]:
                    for j in range(GH):
                        u = GH * n + j
                        pool.wait_ge(g["exp_done"], u + 1)
                        blk = probs[:, u % P_SLOTS, 0:P]
                        nc.gpsimd.affine_select(out=blk, in_=blk, compare_op=ALU.is_ge, fill=0.0, base=0,
                                                pattern=[[1, P]], channel_multiplier=-1).then_inc(g["masked"], 1)

        @block.sync
        def _(sp):
            for i, (group, c) in enumerate(ITEMS):
                if i == 1:
                    for m in (NU * NCH - 2 * KD, NU * NCH - KD):
                        load_stack(sp, m, qs, ks, scratch, stored, stacked)
                sp.wait_ge(g["smax_read"], smax_at[("T", i)] + 1)
                for r in range(2):
                    dst = qs[KS + r:KS + r + 1, c, GH * group:GH * group + GH, :].rearrange("p j (b q) -> p (j b) q", q=P)
                    sp.dma_start(dst, mrow[GH * TPC * r:GH * TPC * (r + 1), :]).then_inc(g["max_row"], 16)
            sp.wait_ge(g["max_row"], ROWS_IN * len(ITEMS))
    clear(nc, list(g.values()))


def build_weights(nc, c, w, loaded, o_all):
    resid = w["resid"]
    with ExitStack() as ctx:
        def sb(name, shape, dt=fp32):
            return ctx.enter_context(nc.sbuf_tensor(name, shape, dt))

        assert nc.sbuf_base == w["raw_at"]
        sb("raw_room", [P, w["raw_room"] // 4])
        wv, upT, downT, woutT, su, sud, sdp = (w[n] for n in ("wv_raw", "upT", "downT", "woutT", "su", "sud", "sdp"))
        fly = [sb(f"fly{i}", [P, KF, D]) for i in range(2)]
        negh = sb("negh", [P, P])
        sud32 = sb("sud32", [P, KF])
        xh, xT, stats, mv, rstd = (w[n] for n in ("xh", "xT", "stats", "mv", "rstd"))
        ps = [ctx.enter_context(nc.psum_tensor(f"wps{i}", [P, CH], fp32)) for i in range(8)]
        names = ["neg", "scales", "pe_done", "copied", "high", "read", "level", "dn_high", "dn_low", "wo_high", "wo_low",
                 "stats_done", "aggregated", "eps_added", "rstd_done", "normed"]
        g = {n: ctx.enter_context(nc.semaphore("w_" + n)) for n in names}
        HD = KF // 2
        jobs = [("hd", f, 0) for f in range(0, KF, 2)] + [("ab", 0, 0)]
        hu = [("hu", a, f) for a in range(KD) for f in range(2 * INTER // CH)]
        for t in range(NCH + 1):
            if t < NCH:
                jobs += [("ot", t, k) for k in range(KD)]
            jobs += [hu.pop(0) for _ in range(2) if hu]
            if t == NCH:
                jobs += [("xt", 0, k) for k in range(KD)]
            if t:
                jobs += [("wo", t - 1, h) for h in range(TPC // 2)]
        split = [n for n, j in enumerate(jobs) if j[0] in ("ab", "ot", "hu", "xt")]
        read = {n: i + 1 for i, n in enumerate(n for n, j in enumerate(jobs) if j[0] != "hd")}
        oT = [[sb(f"oT{i}{p}", [P, KD, CH], fp32r) for p in range(2)] for i in range(2)]

        def target(n):
            kind, a, b = jobs[n]
            if kind == "ot":
                return [t[:, b, :] for t in oT[a % 2]]
            if kind == "xt":
                return [t[:, b, :] for t in xT[a]]
            return [w["ug"][i][:, a, CH * b:CH * b + CH] if kind == "hu" else w["ab"][i][:] for i in range(2)]

        assert nc.sbuf_base <= w["shared_at"]
        added = jobs.index(("wo", 0, TPC // 2 - 1))
        with nc.Block() as block:
            @block.tensor
            def _(pe):
                for n, (kind, a, b) in enumerate(jobs):
                    if n >= 8 + HD:
                        pe.wait_ge(g["read"], read[n - 8])
                    elif n >= 8:
                        pe.wait_ge(g["copied"], n - 8 + 1)
                    bank = ps[n % 8]
                    if kind == "hd":
                        last = nc.tensor.matmul(bank[:], c["hadamard"][:], downT[:, a:a + 2, :].rearrange("p k n -> p (k n)"),
                                                start=True, stop=True)
                    elif kind == "ab":
                        for m in range(KD):
                            for k in range(KD):
                                last = nc.tensor.matmul(bank[:, D * m:D * m + D], wv[:, k, P * m:P * m + P], woutT[:, k, :],
                                                        start=(k == 0), stop=(k == KD - 1))
                    elif kind == "ot":
                        for i in range(TPC):
                            last = nc.tensor.transpose(bank[:, P * i:P * i + P], o_all[:, TPC * a + i, P * b:P * b + P], c["ident"][:])
                    elif kind == "xt":
                        pe.wait_ge(g["normed"], TPC)
                        for i in range(TPC):
                            last = nc.tensor.transpose(bank[:, P * i:P * i + P], xh[:, i, P * b:P * b + P], c["ident"][:])
                    elif kind == "wo":
                        pe.wait_ge(g["read"], read[jobs.index(("ot", a, KD - 1))])
                        pe.wait_ge(g["wo_low"], 1)
                        steps = [(k, i, j) for k in range(KD) for i, j in PASSES]
                        for t in range(2):
                            at = P * (2 * b + t)
                            for m, (k, i, j) in enumerate(steps):
                                last = nc.tensor.matmul(bank[:, D * t:D * t + D], oT[a % 2][i][:, k, at:at + P], w["wo"][j][:, k, :],
                                                        start=(m == 0), stop=(m == len(steps) - 1))
                    else:
                        pe.wait_ge(g["neg"], 1)
                        for k in range(KD):
                            h = negh if a and k else c["hadamard"]
                            last = nc.tensor.matmul(bank[:], h[:], upT[:, k, CH * b:CH * b + CH], start=(k == 0), stop=(k == KD - 1))
                    last.then_inc(g["pe_done"], 1)

            @block.scalar
            def _(act):
                act.wait_ge(loaded["wo"], 16)
                nc.scalar.copy(w["wo"][0][:], w["wo_raw"][:]).then_inc(g["wo_high"], 1)
                act.wait_ge(loaded["small"], 64)
                for n, (kind, a, b) in enumerate(jobs):
                    if n in split:
                        high = target(n)[0]
                        act.wait_ge(g["pe_done"], n + 1)
                        if kind == "ot" and a >= 2:
                            act.wait_ge(g["pe_done"], jobs.index(("wo", a - 2, TPC // 2 - 1)) + 1)
                        nc.scalar.activation(high, _like(ps[n % 8][:], high), ACT.Identity,
                                             scale=su[:, a:a + 1] if kind == "hu" else 1.0).then_inc(g["high"], 1)
                    if n == HD + 8:
                        act.wait_ge(g["level"], 6)
                        act.wait_ge(g["scales"], 2)
                        for f in range(KF):
                            nc.scalar.activation(w["dn"][0][:, f, :], fly[1][:, f, :], ACT.Identity,
                                                 scale=sud32[:, f:f + 1]).then_inc(g["dn_high"], 1)

            @block.vector
            def _(dve):
                nc.vector.tensor_scalar(negh[:], c["hadamard"][:], -1.0, None, ALU.mult).then_inc(g["neg"], 1)
                dve.wait_ge(loaded["small"], 64)
                nc.vector.tensor_scalar(w["gain"][:], w["gains"][:], 1.0 / D ** 0.5, None, ALU.mult).then_inc(g["scales"], 1)
                nc.vector.tensor_scalar(sud32[:], sud[:], 1.0 / INTER ** 0.5, None, ALU.mult).then_inc(g["scales"], 1)
                for n in range(HD):
                    dve.wait_ge(g["pe_done"], n + 1)
                    nc.vector.tensor_tensor(fly[0][:, 2 * n:2 * n + 2, :], ps[n][:].rearrange("p (f n) -> p f n", f=2),
                                            sdp[:].unsqueeze(1).to_broadcast([P, 2, D]), ALU.mult).then_inc(g["copied"], 1)
                dve.wait_ge(g["copied"], HD)
                src, width, count = 0, 1, 0
                while width < KF:
                    if count:
                        dve.wait_ge(g["level"], count)
                    s = fly[src][:].rearrange("p (a two h) n -> p a two (h n)", two=2, h=width)
                    d = fly[1 - src][:].rearrange("p (a two h) n -> p a two (h n)", two=2, h=width)
                    nc.vector.tensor_tensor(d[:, :, 0, :], s[:, :, 0, :], s[:, :, 1, :], ALU.add).then_inc(g["level"], 1)
                    nc.vector.tensor_tensor(d[:, :, 1, :], s[:, :, 0, :], s[:, :, 1, :], ALU.subtract).then_inc(g["level"], 1)
                    src, width, count = 1 - src, 2 * width, count + 2
                dve.wait_ge(loaded["resid"], 16 * NCH)
                for n in range(HD, len(jobs)):
                    kind, a, b = jobs[n]
                    bank = ps[n % 8]
                    if n == added + 4:
                        dve.wait_ge(g["rstd_done"], 1)
                        for t in range(TPC):
                            nc.vector.tensor_scalar(xh[:, t, :], resid[:, t, :], mv[:, t, 0:1], rstd[:, t, 1:2],
                                                    ALU.subtract, ALU.mult).then_inc(g["normed"], 1)
                    if n == len(jobs) - 8:
                        for f in range(KF):
                            dve.wait_ge(g["dn_high"], f + 1)
                            nc.vector.scalar_tensor_tensor(out=w["dn"][1][:, f, :], in0=fly[1][:, f, :], scalar=sud32[:, f:f + 1],
                                                           in1=w["dn"][0][:, f, :].bitcast(fp32), op0=ALU.mult, op1=ALU.subtract)\
                                .then_inc(g["dn_low"], 1)
                    if kind == "wo":
                        at = slice(TPC * a + 2 * b, TPC * a + 2 * b + 2)
                        dve.wait_ge(g["pe_done"], n + 1)
                        nc.vector.tensor_tensor(resid[:, at, :], resid[:, at, :], bank[:].rearrange("p (t n) -> p t n", t=2), ALU.add)\
                            .then_inc(g["read"], 1)
                        if n == added:
                            dve.wait_ge(g["read"], read[n])
                            for t in range(TPC):
                                nc.vector.bn_stats(stats[:, t, :], resid[:, t, :]).then_inc(g["stats_done"], 1)
                            for t in range(TPC):
                                dve.wait_ge(g["stats_done"], t + 1)
                                nc.vector.bn_aggr(mv[:, t, :], stats[:, t, :]).then_inc(g["aggregated"], 1)
                        continue
                    high, low = target(n)
                    dve.wait_ge(g["high"], split.index(n) + 1)
                    if kind == "hu":
                        nc.vector.scalar_tensor_tensor(out=low, in0=bank[:], scalar=su[:, a:a + 1], in1=high.bitcast(fp32),
                                                       op0=ALU.mult, op1=ALU.subtract).then_inc(g["read"], 1)
                    else:
                        nc.vector.tensor_tensor(low, _like(bank[:], low), high.bitcast(fp32), ALU.subtract).then_inc(g["read"], 1)

            @block.gpsimd
            def _(pool):
                pool.wait_ge(g["wo_high"], 1)
                nc.gpsimd.tensor_tensor(w["wo"][1][:], w["wo_raw"][:], w["wo"][0][:].bitcast(fp32), ALU.subtract).then_inc(g["wo_low"], 1)
                pool.wait_ge(g["aggregated"], TPC)
                nc.gpsimd.tensor_scalar(rstd[:, :, 0], mv[:, :, 1], EPS, None, ALU.add).then_inc(g["eps_added"], 1)
                pool.wait_ge(g["eps_added"], 1)
                nc.gpsimd.tensor_tensor(rstd[:, :, 1], rstd[:, :, 0], c["rootexp"][:], ALU.pow).then_inc(g["rstd_done"], 1)
        clear(nc, list(g.values()))


def _like(flat, shaped):
    if len(shaped.shape) == 3:
        return flat.rearrange("p (a b) -> p a b", a=shaped.shape[1])
    return flat


PAIR = 2


def build_layers(nc, ctx, out, c, w, loop):
    def sb(name, shape, dt=fp32):
        return ctx.enter_context(nc.sbuf_tensor(name, shape, dt))

    mid = [[sb(f"mid{i}{p}", [P, KF, CH], fp32r) for p in range(2)] for i in range(PAIR)]
    silu = sb("silu", [P, 2, CH])
    prod = sb("prod", [P, 2, CH])
    psT = ctx.enter_context(nc.psum_tensor("psT2", [P, KD, CH], fp32))
    gate = [ctx.enter_context(nc.psum_tensor(f"gate{i}", [P, CH], fp32)) for i in range(2)]
    up = [ctx.enter_context(nc.psum_tensor(f"up{i}", [P, CH], fp32)) for i in range(2)]
    add = [ctx.enter_context(nc.psum_tensor(f"add{i}", [P, 2, D], fp32)) for i in range(2)]
    resid, xh, xT, stats, mv, rstd = (w[n] for n in ("resid", "xh", "xT", "stats", "mv", "rstd"))
    assert nc.sbuf_base <= w["shared_at"]
    names = ["add_done", "added", "stats_done", "aggregated", "eps_added", "rstd_done", "normed",
             "transposed", "high", "low", "gate_done", "up_done", "silu_done", "prod_done", "mid_high", "mid_low"]
    g = {n: ctx.enter_context(nc.semaphore("l_" + n)) for n in names}
    stored = ctx.enter_context(nc.semaphore("out_stored"))

    assert NCH == 2 * PAIR
    work = [("up", 0), ("down", 0), ("up", 1), ("attn", 0), ("down", 1), ("up", 0), ("attn", 1),
            ("down", 0), ("up", 1), ("down", 1), ("next", 0)]
    ADDS = TPC // 2
    parts_of = [{"up": KF, "next": 0}.get(k, ADDS) for k, _ in work]
    adders = [n for n, (k, _) in enumerate(work) if k in ("down", "attn")]
    users = [n for n, (k, _) in enumerate(work) if k != "down" and n]
    ups = [n for n, (k, _) in enumerate(work) if k == "up"]
    norm_no, turn_no, add_no, up_no = ({n: i for i, n in enumerate(x)} for x in (users, users, adders, ups))

    def last_step(n, kinds):
        found = [m for m in range(n) if work[m][1] == work[n][1] and work[m][0] in kinds]
        return found[-1] if found else None

    first = [n for n in users if last_step(n, ("down", "attn")) is None]
    events, norms = [("norm", n) for n in first], []
    for n, (kind, i) in enumerate(work):
        for p in range(parts_of[n]):
            if p == parts_of[n] - (2 if kind == "up" else 1) and n + 1 in turn_no:
                if n + 1 in norms:
                    events.append(("norm", norms.pop(norms.index(n + 1))))
                events.append(("turn", n + 1))
            events.append(("part", n, p))
        if n in add_no:
            norms += [u for u in users if u > n and last_step(u, ("down", "attn")) == n]
        while norms and (norm_no[norms[0]] == 0 or ("turn", users[norm_no[norms[0]] - 1]) in events):
            events.append(("norm", norms.pop(0)))
    assert not norms
    assert [e[1] for e in events if e[0] == "norm"] == users and [e[1] for e in events if e[0] == "turn"] == users

    def body(pair):
        def tile(i, t, other=False):
            return ((pair * -PAIR + PAIR if other else pair * PAIR) + i) * TPC + t

        def tiles(i, t, n):
            a = tile(i, t)
            return slice(a, a + n) if isinstance(pair, int) else bass.ds(a, n)

        with nc.Block() as block:
            @block.tensor
            def _(pe):
                def turn(n):
                    k0 = turn_no[n]
                    if k0:
                        pe.wait_ge(g["low"], k0)
                    for t in range(TPC):
                        pe.wait_ge(g["normed"], TPC * norm_no[n] + t + 1)
                        for k in range(KD):
                            last = nc.tensor.transpose(psT[:, k, P * t:P * t + P], xh[:, t, P * k:P * k + P], c["ident"][:])
                    last.then_inc(g["transposed"], 1)

                def up_part(n, f):
                    i, u = work[n][1], KF * up_no[n] + f
                    if u >= 2:
                        pe.wait_ge(g["prod_done"], u - 1)
                    for which, banks, sem in ((1, gate, "gate_done"), (0, up, "up_done")):
                        steps = [(k, a, b) for k in range(KD) for a, b in PASSES]
                        for m, (k, a, b) in enumerate(steps):
                            at = INTER * which + P * f
                            last = nc.tensor.matmul(banks[u % 2][:], w["ug"][a][:, k, at:at + P], xT[i][b][:, k, :],
                                                    start=(m == 0), stop=(m == len(steps) - 1))
                        last.then_inc(g[sem], 1)

                def add_part(n, h):
                    kind, i = work[n]
                    left, right, kt = {"down": (mid[i], w["dn"], KF),
                                       "attn": (xT[i], w["ab"], KD)}[kind]
                    r = ADDS * add_no[n] + h
                    if r >= 2:
                        pe.wait_ge(g["added"], r - 1)
                    for t in range(2):
                        at = P * (2 * h + t)
                        steps = [(k, a, b) for k in range(kt) for a, b in PASSES]
                        for m, (k, a, b) in enumerate(steps):
                            if kind == "down" and h == t == 0 and m % len(PASSES) == 0:
                                pe.wait_ge(g["mid_low"], KF * up_no[last_step(n, ("up",))] + k + 1)
                            last = nc.tensor.matmul(add[r % 2][:, t, :], left[a][:, k, at:at + P], right[b][:, k, :],
                                                    start=(m == 0), stop=(m == len(steps) - 1))
                    last.then_inc(g["add_done"], 1)

                for e in events:
                    if e[0] == "turn":
                        turn(e[1])
                    elif e[0] == "part":
                        if e[2] == 0 and e[1] in turn_no:
                            pe.wait_ge(g["low"], turn_no[e[1]] + 1)
                        (up_part if work[e[1]][0] == "up" else add_part)(e[1], e[2])

            @block.scalar
            def _(act):
                def high_part(n):
                    act.wait_ge(g["transposed"], turn_no[n] + 1)
                    before = last_step(n, ("up", "attn"))
                    if before is not None:
                        if work[before][0] == "up":
                            act.wait_ge(g["up_done"], KF * (up_no[before] + 1))
                        else:
                            act.wait_ge(g["add_done"], ADDS * (add_no[before] + 1))
                    nc.scalar.copy(xT[work[n][1]][0][:], psT[:]).then_inc(g["high"], 1)

                def high_mid(n, f):
                    u = KF * up_no[n] + f
                    act.wait_ge(g["prod_done"], u + 1)
                    nc.scalar.copy(mid[work[n][1]][0][:, f, :], prod[:, u % 2, :]).then_inc(g["mid_high"], 1)

                for e in events:
                    if e[0] == "turn":
                        high_part(e[1])
                    elif e[0] == "part" and work[e[1]][0] == "up":
                        _, n, f = e
                        u = KF * up_no[n] + f
                        before = last_step(n, ("down",))
                        if f == 0 and before is not None:
                            act.wait_ge(g["add_done"], ADDS * (add_no[before] + 1))
                        act.wait_ge(g["gate_done"], u + 1)
                        if u >= 2:
                            act.wait_ge(g["prod_done"], u - 1)
                        nc.scalar.activation(silu[:, u % 2, :], gate[u % 2][:], ACT.Silu,
                                             scale=w["gain"][:, KF + f:KF + f + 1]).then_inc(g["silu_done"], 1)
                        if f:
                            high_mid(n, f - 1)
                        if f == KF - 1:
                            high_mid(n, f)

            @block.gpsimd
            def _(pool):
                for e in events:
                    if e[0] == "norm":
                        k0 = norm_no[e[1]]
                        pool.wait_ge(g["aggregated"], TPC * (k0 + 1))
                        nc.gpsimd.tensor_scalar(rstd[:, :, 0], mv[:, :, 1], EPS, None, ALU.add).then_inc(g["eps_added"], 1)
                        pool.wait_ge(g["eps_added"], k0 + 1)
                        nc.gpsimd.tensor_tensor(rstd[:, :, 1], rstd[:, :, 0], c["rootexp"][:], ALU.pow).then_inc(g["rstd_done"], 1)
                    elif e[0] == "part" and work[e[1]][0] == "up":
                        i, f = work[e[1]][1], e[2]
                        u = KF * up_no[e[1]] + f
                        pool.wait_ge(g["mid_high"], u + 1)
                        nc.gpsimd.tensor_tensor(mid[i][1][:, f, :], prod[:, u % 2, :], mid[i][0][:, f, :].bitcast(fp32),
                                                ALU.subtract).then_inc(g["mid_low"], 1)

            @block.vector
            def _(dve):
                def norm(n):
                    k0, i = norm_no[n], work[n][1]
                    before = last_step(n, ("down", "attn"))
                    if before is not None:
                        dve.wait_ge(g["added"], ADDS * (add_no[before] + 1))
                    if k0:
                        dve.wait_ge(g["normed"], TPC * k0)
                    for t in range(TPC):
                        nc.vector.bn_stats(stats[:, t, :], resid[:, tile(i, t, work[n][0] == "next"), :]).then_inc(g["stats_done"], 1)
                    for t in range(TPC):
                        dve.wait_ge(g["stats_done"], TPC * k0 + t + 1)
                        nc.vector.bn_aggr(mv[:, t, :], stats[:, t, :]).then_inc(g["aggregated"], 1)
                    dve.wait_ge(g["rstd_done"], k0 + 1)
                    if k0:
                        dve.wait_ge(g["transposed"], turn_no[users[k0 - 1]] + 1)
                    for t in range(TPC):
                        nc.vector.tensor_scalar(xh[:, t, :], resid[:, tile(i, t, work[n][0] == "next"), :], mv[:, t, 0:1],
                                                rstd[:, t, 1:2], ALU.subtract, ALU.mult).then_inc(g["normed"], 1)

                for e in events:
                    if e[0] == "norm":
                        norm(e[1])
                    elif e[0] == "turn":
                        dve.wait_ge(g["high"], turn_no[e[1]] + 1)
                        x = xT[work[e[1]][1]]
                        nc.vector.tensor_tensor(x[1][:], psT[:], x[0][:].bitcast(fp32), ALU.subtract).then_inc(g["low"], 1)
                    elif work[e[1]][0] == "up":
                        _, n, f = e
                        u = KF * up_no[n] + f
                        dve.wait_ge(g["silu_done"], u + 1)
                        dve.wait_ge(g["up_done"], u + 1)
                        if u >= 2:
                            dve.wait_ge(g["mid_low"], u - 1)
                        nc.vector.scalar_tensor_tensor(out=prod[:, u % 2, :], in0=up[u % 2][:], scalar=w["gain"][:, f:f + 1],
                                                       in1=silu[:, u % 2, :], op0=ALU.mult, op1=ALU.mult)\
                            .then_inc(g["prod_done"], 1)
                    else:
                        _, n, h = e
                        r = ADDS * add_no[n] + h
                        dve.wait_ge(g["add_done"], r + 1)
                        at = tiles(work[n][1], 2 * h, 2)
                        nc.vector.tensor_tensor(resid[:, at, :], resid[:, at, :], add[r % 2][:], ALU.add).then_inc(g["added"], 1)

            @block.sync
            def _(sp):
                for i in range(PAIR):
                    last = max(a for a in adders if work[a][1] == i)
                    sp.wait_ge(g["added"], ADDS * (add_no[last] + 1))
                    rows = out[0].rearrange("(t p) d -> p t d", p=P)
                    sp.dma_start(rows[:, tiles(i, 0, TPC), :], resid[:, tiles(i, 0, TPC), :]).then_inc(stored, 16)
        clear(nc, list(g.values()))

    if loop:
        with nc.Fori(0, NCH // PAIR) as pair:
            body(pair)
    else:
        for pair in range(NCH // PAIR):
            body(pair)
    with nc.Block() as block:
        @block.sync
        def _(sp):
            sp.wait_ge(stored, 16 * NCH)


def build(nc, x, w_q, w_k, w_v, w_o, weight_qkv, weight_out, SU_ug, SU_dp, Wscale_ug, Wscale_dp, W_up, W_gate, W_down, out,
          loop_layers=True):
    ins = dict(x=x, w_o=w_o, weight_qkv=weight_qkv, weight_out=weight_out, SU_ug=SU_ug, SU_dp=SU_dp,
               Wscale_ug=Wscale_ug, Wscale_dp=Wscale_dp, W_up=W_up, W_gate=W_gate, W_down=W_down)
    with ExitStack() as ctx:
        def sb(name, shape, dt=fp32, ctx=ctx):
            return ctx.enter_context(nc.sbuf_tensor(name, shape, dt))

        ident = sb("ident", [P, P])
        identb = sb("identb", [P, P], bf16)
        causal = sb("causal", [P, P], bf16)
        hadamard = sb("hadamard", [P, P])
        rootexp = sb("rootexp", [P, TPC])
        o_all = sb("o_all", [P, TILES, D])
        w = {n: sb(n, shape) for n, shape in (("gains", [P, 2 * KF]), ("gain", [P, 2 * KF]), ("su", [P, KD]), ("sud", [P, KF]),
                                              ("sdp", [P, D]))}
        base = nc.sbuf_base
        kept = [("resid", [P, TILES, D]), ("wo_raw", [P, KD, D])]
        made = [("ug", [P, KD, 2 * INTER]), ("dn", [P, KF, D]), ("ab", [P, KD, D]), ("wo", [P, KD, D])]
        raws = [("up_raw", [P, 2 * KF, D]), ("down_raw", [P, KD, INTER]), ("wv_raw", [P, KD, D]),
                ("wout_raw", [P, KD, D]), ("downT", [P, KF, D]), ("woutT", [P, KD, D])]

        def room(tensors):
            return sum(-(-4 * math.prod(shape[1:]) // 32) * 32 for _, shape in tensors)

        kept_at = base + 2 * room(made)
        raw_at = kept_at + room(kept)
        w.update(up_at=nc.sbuf_top - 4 * KD * 2 * INTER, raw_at=raw_at, raw_room=room(raws))
        for at, tensors in ((kept_at, kept), (raw_at, raws)):
            for i, (name, shape) in enumerate(tensors):
                w[name] = nc.alloc_sbuf_tensor_at(name, shape, fp32, offset=at + room(tensors[:i]))
        w["upT"] = nc.alloc_sbuf_tensor_at("upT", [P, KD, 2 * INTER], fp32, offset=w["up_at"])
        chunk_bytes, head_bytes = 2 * HEADS * CH, 2 * S
        assert kept_at >= base + (NCH - 1) * chunk_bytes and raw_at >= base + HEADS * head_bytes
        assert raw_at + room(raws) <= base + (HEADS + HEADS - GH) * head_bytes
        loaded = {n: ctx.enter_context(nc.semaphore("loaded_" + n)) for n in ("up", "down", "attn", "wo", "small", "resid")}
        with ExitStack() as attn:
            qs = sb("qs", [KM, NCH, HEADS, CH], bf16, attn)
            ks = sb("ks", [KM, HEADS, S], bf16, attn)
            v_aug = sb("v_aug", [P, TILES, HEADS, VW], fp32, attn)
            ones = o_all[:, TILES - 1, :].bitcast(bf16)
            stacked = [ctx.enter_context(nc.semaphore(f"stacked{c}")) for c in range(NCH)]
            stored = [ctx.enter_context(nc.semaphore(f"stored{i}")) for i in range(SLOTS)]
            scratch = nc.dram_tensor("qk_parts", (2, PARTS, D, S), bf16).ap()
            own = o_all[:].rearrange("p t d -> p (t d)").bitcast(bf16)
            lent_at = base + 2 * (NCH - 1) * HEADS * CH
            spare_xT = [nc.alloc_sbuf_tensor_at(f"spare_xT{i}", [P, KD, CH], fp32r, offset=lent_at + 4 * KD * CH * i) for i in range(2)]
            lent = nc.alloc_sbuf_tensor_at("lent_parts", [P, len(LENT_SLOTS) * PARTS * CH], bf16, offset=lent_at + 8 * KD * CH)

            def parts(n):
                slot = n % SLOTS
                at, room = (OWN_SLOTS.index(slot), own) if slot in OWN_SLOTS else (LENT_SLOTS.index(slot), lent[:])
                return room[:, PARTS * CH * at:PARTS * CH * (at + 1)].rearrange("p (a n) -> p a n", a=PARTS)

            build_projections(nc, x, w_q, w_k, w_v, dict(ident=ident, identb=identb, causal=causal,
                                                         rootexp=rootexp, ones=ones),
                              qs, ks, v_aug, parts, spare_xT, stacked, stored, scratch, lambda: load_vectors(nc, ins, w, loaded))
            build_attention(nc, attn, dict(qs=qs, ks=ks, v_aug=v_aug, o_all=o_all, ident=ident, identb=identb,
                                           causal=causal, hadamard=hadamard, parts=parts), stacked, stored, scratch,
                            later_loads(ins, w), loaded, w)
        c = dict(ident=ident, hadamard=hadamard, rootexp=rootexp)
        assert nc.sbuf_base == base
        for name, shape in made:
            w[name] = [sb(f"{name}{i}", shape, fp32r) for i in range(2)]
        assert nc.sbuf_base == kept_at
        sb("kept_room", [P, room(kept) // 4])
        shared = [("xh", [P, TPC, D], fp32), ("stats", [P, TPC, 6], fp32), ("mv", [P, TPC, 2], fp32), ("rstd", [P, TPC, 2], fp32)]
        shared += [(f"lxT{i}{p}", [P, KD, CH], fp32r) for i in range(PAIR) for p in range(2)]
        sizes = [(name, shape) for name, shape, _ in shared]
        w["shared_at"] = w["up_at"] - room(sizes)
        for i, (name, shape, dt) in enumerate(shared):
            w[name] = nc.alloc_sbuf_tensor_at(name, shape, dt, offset=w["shared_at"] + room(sizes[:i]))
        w["xT"] = [[w[f"lxT{i}{p}"] for p in range(2)] for i in range(PAIR)]
        build_weights(nc, c, w, loaded, o_all)
        build_layers(nc, ctx, out, c, w, loop_layers)


_INS = ['L0_attn_a_x', 'L0_attn_a_w_q', 'L0_attn_a_w_k', 'L0_attn_a_w_v', 'L0_attn_a_w_o', 'L0_attn_b_weight_qkv',
        'L0_attn_b_weight_out', 'L0_ffn_SU_ug', 'L0_ffn_SU_dp', 'L0_ffn_Wscale_ug', 'L0_ffn_Wscale_dp', 'L0_ffn_W_up',
        'L0_ffn_W_gate', 'L0_ffn_W_down']


def kernel(**inputs):
    import numpy as _np
    import concourse.bacc as _bacc
    from concourse import mybir as _mybir
    from concourse.bass_utils import run_bass_kernel_spmd as _run

    nc = _bacc.Bacc("TRN2", target_bir_lowering=False, num_devices=1)
    arrays, args = {}, []
    for name in _INS:
        a = _np.ascontiguousarray(inputs[name])
        arrays[f"in_{name}_dram"] = a
        args.append(nc.dram_tensor(f"in_{name}_dram", a.shape, _mybir.dt.from_np(a.dtype), kind="ExternalInput").ap())
    out = nc.dram_tensor("out_0_dram", (1, S, D), fp32, kind="ExternalOutput").ap()
    build(nc, *args, out)
    r = _run(nc, [arrays], core_ids=[0])
    return r.results[0]["out_0_dram"]
```
